# Optimizing a Trainium2 kernel written in Bass

```python
import numpy as np
import jax
import jax.numpy as jnp

def _softmax(x, axis=-1):
    return jax.nn.softmax(x, axis=axis)

def _gelu(x):
    return jax.nn.gelu(x, approximate=True)

def _silu(x):
    return jax.nn.silu(x)

def _sigmoid(x):
    return jax.nn.sigmoid(x)

def _layernorm(x, axis=-1, eps=1e-05):
    m = jnp.mean(x, axis=axis, keepdims=True)
    v = jnp.var(x, axis=axis, keepdims=True)
    return (x - m) / jnp.sqrt(v + eps)

def _scatter_add(tgt, idx, src, axis=0):
    return tgt.at[idx].add(src)

def _segment_sum(src, seg, n):
    return jax.ops.segment_sum(src, seg, n)
kernel_name = 'mk_gnn_ffn_d1_gnn_r32_2cafde'

def setup_inputs(seed: int=0):
    np.random.seed(seed)
    _w = jnp.asarray

    def _rec_inputs():
        import jax
        import jax.numpy as jnp
        _gk = jax.random.key(seed)
        x = -6.415e-05 + 1 * jax.random.normal(jax.random.fold_in(_gk, 1), (625, 512), jnp.float32)
        src = jax.random.randint(jax.random.fold_in(_gk, 2), (10000,), 0, 625, jnp.int32)
        dst = jnp.minimum((625 * jax.random.uniform(jax.random.fold_in(_gk, 3), (10000,)) ** 2.0).astype(jnp.int32), 19999)
        _o = jnp.argsort(dst, stable=True)
        src = src[_o]
        dst = dst[_o]
        return (x, src, dst)
    x, src, dst = _rec_inputs()

    def _L0_gnn_setup():
        import jax, jax.numpy as jnp
        import numpy as np
        N = 625
        E_RAND = 4375
        D_IN = 512
        D_OUT = 512
        SLOPE = 0.2
        key = jax.random.key(seed)
        k1, k2, k3, k4 = jax.random.split(key, 4)
        nodes = jax.random.normal(k1, (N, D_IN), dtype=jnp.float32)
        ei = jax.random.randint(k2, (2, E_RAND), 0, N, dtype=jnp.int64)
        loops = jnp.arange(N, dtype=jnp.int64)
        edge_index = jnp.concatenate([ei, jnp.stack([loops, loops])], axis=1)
        W = jax.random.normal(k3, (D_IN, D_OUT), dtype=jnp.float32) * (1.0 / np.sqrt(D_IN))
        b_w = jnp.zeros((D_OUT,), dtype=jnp.float32)
        a = jax.random.normal(k4, (2 * D_OUT,), dtype=jnp.float32) * (1.0 / np.sqrt(2 * D_OUT))
        b_a = jnp.zeros((), dtype=jnp.float32)
        return {'nodes': nodes, 'edge_index': edge_index, 'W': W, 'b_w': b_w, 'a': a, 'b_a': b_a}
    _L0_gnn_all = _L0_gnn_setup()
    _L0_gnn_in = {k: v for k, v in _L0_gnn_all.items() if k in ('W', 'b_w', 'a', 'b_a')}
    del _L0_gnn_all

    def _L0_ffn_setup():
        import jax, jax.numpy as jnp
        import numpy as np
        DIM, DEPTH, MULT = (512, 3, 4)
        E = 2 ** DEPTH
        HID = MULT * DIM
        B, S = (4, 1024)

        def _leaf_probs(flat_x, rw, rb):
            n_tok = flat_x.shape[0]
            leaf = jnp.ones((n_tok, 1), dtype=flat_x.dtype)
            for d in range(DEPTH):
                off, n = (2 ** d - 1, 2 ** d)
                logits = flat_x @ rw[off:off + n].T + rb[off:off + n]
                p = jax.nn.sigmoid(logits)
                leaf = (leaf[:, :, None] * jnp.stack([1.0 - p, p], axis=2)).reshape(n_tok, 2 * n)
            return leaf
        key = jax.random.key(seed)
        ks = jax.random.split(key, 7)
        sd = 1.0 / np.sqrt(DIM)
        sh = 1.0 / np.sqrt(HID)
        return {'x': jax.random.normal(ks[0], (B, S, DIM), dtype=jnp.float32), 'rw': jax.random.normal(ks[1], (E - 1, DIM), dtype=jnp.float32) * sd, 'rb': jax.random.normal(ks[2], (E - 1,), dtype=jnp.float32) * sd, 'w1': jax.random.normal(ks[3], (E, DIM, HID), dtype=jnp.float32) * sd, 'b1': jax.random.normal(ks[4], (E, HID), dtype=jnp.float32) * sd, 'w2': jax.random.normal(ks[5], (E, HID, DIM), dtype=jnp.float32) * sh, 'b2': jax.random.normal(ks[6], (E, DIM), dtype=jnp.float32) * sh}
    _L0_ffn_all = _L0_ffn_setup()
    _L0_ffn_in = {k: v for k, v in _L0_ffn_all.items() if k in ('rw', 'rb', 'w1', 'b1', 'w2', 'b2')}
    del _L0_ffn_all
    return {'x': x, 'src': src, 'dst': dst, 'L0_gnn_W': _L0_gnn_in['W'], 'L0_gnn_b_w': _L0_gnn_in['b_w'], 'L0_gnn_a': _L0_gnn_in['a'], 'L0_gnn_b_a': _L0_gnn_in['b_a'], 'L0_ffn_rw': _L0_ffn_in['rw'], 'L0_ffn_rb': _L0_ffn_in['rb'], 'L0_ffn_w1': _L0_ffn_in['w1'], 'L0_ffn_b1': _L0_ffn_in['b1'], 'L0_ffn_w2': _L0_ffn_in['w2'], 'L0_ffn_b2': _L0_ffn_in['b2']}

def reference(x, src, dst, L0_gnn_W, L0_gnn_b_w, L0_gnn_a, L0_gnn_b_a, L0_ffn_rw, L0_ffn_rb, L0_ffn_w1, L0_ffn_b1, L0_ffn_w2, L0_ffn_b2):
    import jax
    import jax.numpy as jnp

    def _L0_gnn_ref(nodes, edge_index, W, b_w, a, b_a):
        import jax, jax.numpy as jnp
        import numpy as np
        N = 625
        E_RAND = 4375
        D_IN = 512
        D_OUT = 512
        SLOPE = 0.2
        h = nodes @ W + b_w
        src = edge_index[0]
        dst = edge_index[1]
        s_dst = h @ a[:D_OUT]
        s_src = h @ a[D_OUT:]
        e = jax.nn.leaky_relu(s_dst[dst] + s_src[src] + b_a, negative_slope=SLOPE)
        w = jnp.exp(e)
        denom = jax.ops.segment_sum(w, dst, num_segments=N)
        alpha = w / denom[dst]
        out = jax.ops.segment_sum(alpha[:, None] * h[src], dst, num_segments=N)
        return out

    def _L0_ffn_ref(x, rw, rb, w1, b1, w2, b2):
        import jax, jax.numpy as jnp
        import numpy as np
        DIM, DEPTH, MULT = (512, 3, 4)
        E = 2 ** DEPTH
        HID = MULT * DIM
        B, S = (4, 1024)

        def _leaf_probs(flat_x, rw, rb):
            n_tok = flat_x.shape[0]
            leaf = jnp.ones((n_tok, 1), dtype=flat_x.dtype)
            for d in range(DEPTH):
                off, n = (2 ** d - 1, 2 ** d)
                logits = flat_x @ rw[off:off + n].T + rb[off:off + n]
                p = jax.nn.sigmoid(logits)
                leaf = (leaf[:, :, None] * jnp.stack([1.0 - p, p], axis=2)).reshape(n_tok, 2 * n)
            return leaf
        b, s, dim = x.shape
        flat_x = x.reshape(b * s, dim)
        leaf_probs = _leaf_probs(flat_x, rw, rb)
        h = jnp.einsum('nd,edh->neh', flat_x, w1) + b1[None]
        h = jax.nn.gelu(h, approximate=False)
        y = jnp.einsum('neh,ehd->ned', h, w2) + b2[None]
        out = jnp.einsum('ned,ne->nd', y, leaf_probs)
        return out.reshape(b, s, dim)
    edge_index = jnp.stack([src, dst])
    x = x + _L0_gnn_ref(_layernorm(x, axis=-1), edge_index, L0_gnn_W, L0_gnn_b_w, L0_gnn_a, L0_gnn_b_a)
    x = x + _L0_ffn_ref(_layernorm(x, axis=-1)[None], L0_ffn_rw, L0_ffn_rb, L0_ffn_w1, L0_ffn_b1, L0_ffn_w2, L0_ffn_b2)[0]
    return x

_drawn_inputs = setup_inputs


def setup_inputs(seed=0):
    import zlib

    import numpy as np

    out = dict(_drawn_inputs(seed))
    spreads = {'L0_gnn_b_w': (0.0, 0.1)}
    factors = {'L0_ffn_rb': 8.0, 'L0_ffn_b1': 4.556, 'L0_ffn_b2': 6.472}
    for name, (base, spread) in spreads.items():
        noise = np.random.default_rng([zlib.crc32(name.encode()), seed]).standard_normal(out[name].shape)
        drawn = base * np.exp(spread * noise) if base else spread * noise
        out[name] = jnp.asarray(drawn.astype(out[name].dtype))
    for name, factor in factors.items():
        out[name] = (out[name] * factor).astype(out[name].dtype)
    return out
```

```python
from contextlib import ExitStack

import concourse.bass as bass
from concourse import mybir

ALU = mybir.AluOpType
ACT = mybir.ActivationFunctionType
F32 = mybir.dt.float32
F32R = mybir.dt.float32r
F16 = mybir.dt.float16
I32 = mybir.dt.int32

P = 128
N = 625
TB = 125
NB = N // TB
D = 512
DK = D // P
E = 8
HID = 2048
HT = HID // P
CW = 512
CH = HID // CW
TC = CW // P
NP = N + 1
HALVES = ((0, 314), (314, 312))
UNITS = 2 * HT
PIECES = DK + TC
EPS = 1e-5
SLOPE = 0.2
FLT_MAX = 3.4028234663852886e38

EDGES = 10000
EC = EDGES // TB
LO_N = 313
OW = 314
SW = 626
FIELD = 4096.0
FIELD_BITS = 12
OH_SLOTS = 4
GROUPS = (28, 28, 24)
CONSTS = 7
assert sum(GROUPS) == EC and max(GROUPS) * TB < FIELD and all(g % OH_SLOTS == 0 for g in GROUPS)



def gnn_ffn_kernel(nc, x, src, dst, w_gnn, b_w, a_vec, b_a, rw_t, rb, w1, b1_t, w2, b2, out):
    with ExitStack() as ctx:
        def sb(scope, name, shape, dt=F32):
            return scope.enter_context(nc.sbuf_tensor(name, shape, dt))

        def sem(name):
            return ctx.enter_context(nc.semaphore(name))

        y_ps = ctx.enter_context(nc.psum_tensor("y_ps", [P, NB, 512], F32))
        r_ps = ctx.enter_context(nc.psum_tensor("r_ps", [P, 3, 512], F32))

        acc = sb(ctx, "acc", [TB, NB, D])
        xn = sb(ctx, "xn", [TB, NB, D])
        xt_hi = sb(ctx, "xt_hi", [P, DK, NP], F32R)
        xt_lo = sb(ctx, "xt_lo", [P, DK, NP], F32R)
        ident = sb(ctx, "ident", [P, P])
        stats = sb(ctx, "stats", [TB, NB, 6])
        moments = sb(ctx, "moments", [TB, NB, 2])
        var_eps = sb(ctx, "var_eps", [TB, NB])
        minus_half = sb(ctx, "minus_half", [TB, NB])
        rstd = sb(ctx, "rstd", [TB, NB])
        leaf = sb(ctx, "leaf", [TB, NB, E])
        rwt = sb(ctx, "rwt", [P, DK, 8])
        rwt_hi = sb(ctx, "rwt_hi", [P, DK, 8], F32R)
        rwt_lo = sb(ctx, "rwt_lo", [P, DK, 8], F32R)
        rb_bc = sb(ctx, "rb_bc", [TB, 7])
        logits = sb(ctx, "logits", [TB, NB, 7])
        e_neg = sb(ctx, "e_neg", [TB, NB, 7])
        prob = sb(ctx, "prob", [TB, NB, 7, 2])
        pair = sb(ctx, "pair", [TB, NB, 4])
        b1_sb = sb(ctx, "b1_sb", [P, E * HT])
        b1_now = sb(ctx, "b1_now", [P, HT])
        b2_bc = sb(ctx, "b2_bc", [TB, E, D])
        w_raw = [sb(ctx, "w_raw0", [P, PIECES, CW])]
        w_hi = [sb(ctx, "w_hi0", [P, PIECES, CW], F32R)]
        w_lo = [sb(ctx, "w_lo0", [P, PIECES, CW], F32R)]

        with ExitStack() as gnn:
            wg_raw = sb(gnn, "wg_raw", [P, DK, D])
            count = sb(gnn, "count", [TB, NB, N])
            hg_hi = sb(gnn, "hg_hi", [TB, NB, D], F32R)
            hg_lo = sb(gnn, "hg_lo", [TB, NB, D], F32R)
            h32 = sb(gnn, "h32", [TB, 2, D])
            scratch = sb(gnn, "scratch", [TB, D])
            a_bc = sb(gnn, "a_bc", [TB, 2, D])
            bw_bc = sb(gnn, "bw_bc", [TB, D])
            ba_bc = sb(gnn, "ba_bc", [TB, 1])
            s_dst = sb(gnn, "s_dst", [TB, NB])
            s_src = sb(gnn, "s_src", [TB, NB])
            s_src_b = sb(gnn, "s_src_b", [TB, NB])
            s_src_s = sb(gnn, "s_src_s", [TB, NB])
            ones_f = sb(gnn, "ones_f", [TB, TB])
            ones_2 = sb(gnn, "ones_2", [TB, 2], F32)
            ones_r = sb(gnn, "ones_r", [TB, 2], F32R)
            iota_src = sb(gnn, "iota_src", [TB, SW], F16)
            iota_i = sb(gnn, "iota_i", [TB, SW], I32)
            edge_i = sb(gnn, "edge_i", [TB, 2, EC], I32)
            edge_f = sb(gnn, "edge_f", [TB, 2, EC])
            upper = sb(gnn, "upper", [TB, EC])
            dst_lo = sb(gnn, "dst_lo", [TB, EC])
            dst_val = sb(gnn, "dst_val", [TB, EC])
            den = sb(gnn, "den", [TB, NB])
            den_zero = sb(gnn, "den_zero", [TB, NB])
            den_safe = sb(gnn, "den_safe", [TB, NB])
            rden = sb(gnn, "rden", [TB, NB])
            with ExitStack() as early:
                wg_hi = sb(early, "wg_hi", [P, DK, D], F32R)
                wg_lo = sb(early, "wg_lo", [P, DK, D], F32R)
                oh_src = sb(early, "oh_src", [TB, OH_SLOTS, SW], F16)
                oh_dst = sb(early, "oh_dst", [TB, OH_SLOTS, OW], F16)
                packed = sb(early, "packed", [TB, NB, OW], I32)
                cnt_up = sb(early, "cnt_up", [TB, NB, OW], I32)
                cnt_dn = sb(early, "cnt_dn", [TB, NB, OW], I32)
            with ExitStack() as late:
                attn_hi = sb(late, "attn_hi", [TB, NB, N], F32R)
                attn_lo = sb(late, "attn_lo", [TB, NB, N], F32R)
                diag = sb(late, "diag", [TB, NB, TB])
                s_bc = sb(late, "s_bc", [TB, N])
                ex = sb(late, "ex", [TB, 2, 2, N])
        w_raw.append(sb(ctx, "w_raw1", [P, PIECES, CW]))
        w_hi.append(sb(ctx, "w_hi1", [P, PIECES, CW], F32R))
        w_lo.append(sb(ctx, "w_lo1", [P, PIECES, CW], F32R))
        g = sb(ctx, "g", [P, 2, NP])
        h_hi = sb(ctx, "h_hi", [P, 2, NP], F32R)
        h_lo = sb(ctx, "h_lo", [P, 2, NP], F32R)

        x_in = sem("x_in")
        edges_in = sem("edges_in")
        wg_in = sem("wg_in")
        vec_in = sem("vec_in")
        ffn_vec_in = sem("ffn_vec_in")
        w_in = [sem("w_in0"), sem("w_in1")]
        out_written = sem("out_written")
        pool_seq = sem("pool_seq")
        consts_ready = sem("consts_ready")
        iota_ready = sem("iota_ready")
        dve_seq = sem("dve_seq")
        ve_ready = sem("ve_ready")
        rstd_ready = sem("rstd_ready")
        xn_ready = sem("xn_ready")
        tp_done = sem("tp_done")
        xt_hi_ready = sem("xt_hi_ready")
        xt_ready = sem("xt_ready")
        wg_hi_ready = sem("wg_hi_ready")
        wg_ready = sem("wg_ready")
        hg_done = sem("hg_done")
        h32_ready = sem("h32_ready")
        hg_hi_ready = sem("hg_hi_ready")
        hg_ready = sem("hg_ready")
        oh_ready = sem("oh_ready")
        oh_used = sem("oh_used")
        cnt_done = sem("cnt_done")
        packed_ready = sem("packed_ready")
        packed_used = sem("packed_used")
        diag_ready = sem("diag_ready")
        sbc_done = sem("sbc_done")
        sbc_copied = sem("sbc_copied")
        ex_max = sem("ex_max")
        ex_ready = sem("ex_ready")
        attn_ready = sem("attn_ready")
        attn_hi_ready = sem("attn_hi_ready")
        attn_lo_ready = sem("attn_lo_ready")
        agg_done = sem("agg_done")
        den_done = sem("den_done")
        den_read = sem("den_read")
        rt_hi_ready = sem("rt_hi_ready")
        rt_ready = sem("rt_ready")
        router_done = sem("router_done")
        logits_ready = sem("logits_ready")
        e_neg_ready = sem("e_neg_ready")
        w_hi_ready = sem("w_hi_ready")
        w_ready = sem("w_ready")
        b1_ready = sem("b1_ready")
        h_done = sem("h_done")
        gelu_done = sem("gelu_done")
        h_hi_ready = sem("h_hi_ready")
        h_ready = sem("h_ready")
        l2_done = sem("l2_done")
        y_done = sem("y_done")
        y_added = sem("y_added")
        b2_added = sem("b2_added")

        w1_v = w1.rearrange("e (k p) n -> e p k n", p=P)
        w2_v = w2.rearrange("e (t p) n -> e p t n", p=P)

        block = ctx.enter_context(nc.Block())

        @block.sync
        def _(sp):
            sp.dma_start(edge_i[:, 0, :], src.rearrange("(p c) -> p c", c=EC)).then_inc(edges_in, 16)
            sp.dma_start(edge_i[:, 1, :], dst.rearrange("(p c) -> p c", c=EC)).then_inc(edges_in, 16)
            sp.dma_start(acc[:], x.rearrange("(b p) d -> p b d", p=TB)).then_inc(x_in, 16)
            sp.dma_start(wg_raw[:], w_gnn.rearrange("(k p) n -> p k n", p=P)).then_inc(wg_in, 16)
            sp.dma_start(bw_bc[:], b_w.partition_broadcast(TB)).then_inc(vec_in, 16)
            sp.dma_start(a_bc[:, 0, :], a_vec[0:D].partition_broadcast(TB)).then_inc(vec_in, 16)
            sp.dma_start(a_bc[:, 1, :], a_vec[D:2 * D].partition_broadcast(TB)).then_inc(vec_in, 16)
            sp.dma_start(ba_bc[:], b_a.partition_broadcast(TB)).then_inc(vec_in, 16)

            def load_chunk(e, c):
                slot = c % 2
                sp.dma_start(w_raw[slot][:, 0:DK, :], w1_v[bass.ds(e, 1), :, :, c * CW:(c + 1) * CW]
                             .rearrange("e p k n -> p (e k) n")).then_inc(w_in[slot], 16)
                sp.dma_start(w_raw[slot][:, DK:PIECES, :], w2_v[bass.ds(e, 1), :, c * TC:(c + 1) * TC, :]
                             .rearrange("e p t n -> p (e t) n")).then_inc(w_in[slot], 16)

            load_chunk(0, 0)
            sp.wait_ge(consts_ready, CONSTS)
            sp.dma_start(rwt[:, :, 0:7], rw_t.rearrange("p (k n) -> p k n", k=DK)).then_inc(ffn_vec_in, 16)
            sp.dma_start(rb_bc[:], rb.partition_broadcast(TB)).then_inc(ffn_vec_in, 16)
            sp.dma_start(b1_sb[:], b1_t).then_inc(ffn_vec_in, 16)
            sp.dma_start(b2_bc[:].rearrange("p e d -> p (e d)"),
                         b2.rearrange("e d -> (e d)").partition_broadcast(TB)).then_inc(ffn_vec_in, 16)
            sp.wait_ge(agg_done, NB)
            sp.wait_ge(den_read, NB)
            sp.wait_ge(xt_ready, NB + 1)
            load_chunk(0, 1)
            for c in (2, 3):
                sp.wait_ge(w_ready, PIECES * (c - 1))
                load_chunk(0, c)
            with sp.Fori(1, E) as e:
                for c in range(CH):
                    sp.wait_ge(w_ready, e * (CH * PIECES) + PIECES * (c - 1))
                    load_chunk(e, c)
            for b in range(NB):
                sp.wait_ge(y_added, NB * E + b + 1)
                sp.dma_start(out[b * TB:(b + 1) * TB, :], acc[:, b, :]).then_inc(out_written, 16)
            sp.wait_ge(out_written, 16 * NB)

        @block.gpsimd
        def _(pool):
            pool.iota(iota_i[:], [[1, SW]], base=0, channel_multiplier=0).then_inc(pool_seq, 1)
            pool.wait_ge(pool_seq, 1)
            pool.tensor_copy(iota_src[:], iota_i[:]).then_inc(iota_ready, 1)
            pool.memset(ident[:], 0.0).then_inc(pool_seq, 1)
            pool.wait_ge(pool_seq, 2)
            pool.affine_select(out=ident[:], in_=ident[:], compare_op=ALU.not_equal, fill=1.0, base=0,
                               pattern=[[-1, P]], channel_multiplier=1).then_inc(consts_ready, 1)
            pool.memset(minus_half[:], -0.5).then_inc(consts_ready, 1)
            pool.memset(ones_f[:], 1.0).then_inc(consts_ready, 1)
            pool.memset(ones_2[:], 1.0).then_inc(pool_seq, 1)
            pool.wait_ge(pool_seq, 3)
            pool.tensor_copy(ones_r[:], ones_2[:]).then_inc(consts_ready, 1)
            pool.memset(xt_hi[:, :, N:NP].bitcast(F32), 0.0).then_inc(consts_ready, 1)
            pool.memset(xt_lo[:, :, N:NP].bitcast(F32), 0.0).then_inc(consts_ready, 1)
            pool.memset(rwt[:, :, 7:8], 0.0).then_inc(consts_ready, 1)
            pool.wait_ge(consts_ready, CONSTS)
            pool.wait_ge(ve_ready, 1)
            pool.tensor_tensor(rstd[:], var_eps[:], minus_half[:], ALU.pow).then_inc(rstd_ready, 1)
            for b in range(NB):
                pool.wait_ge(ve_ready, 2 + b)
                pool.tensor_tensor(rstd[:, b:b + 1], var_eps[:, b:b + 1], minus_half[:, b:b + 1],
                                   ALU.pow).then_inc(rstd_ready, 1)

        @block.scalar
        def _(act):
            act.wait_ge(wg_in, 16)
            for k in range(DK):
                act.activation(wg_hi[:, k, :], wg_raw[:, k, :], ACT.Copy).then_inc(wg_hi_ready, 1)

            def transposed_hi(first):
                for b in range(NB):
                    act.wait_ge(tp_done, first + b + 1)
                    act.activation(xt_hi[:, :, b * TB:(b + 1) * TB],
                                   r_ps[:, TP_BANK[first + b], 0:DK * TB].rearrange("p (k n) -> p k n", k=DK),
                                   ACT.Copy).then_inc(xt_hi_ready, 1)

            def counts_to_int(gr):
                for jb in range(NB):
                    if jb < NB - 1:
                        act.wait_ge(cnt_done, (NB - 1) * gr + jb + 1)
                    else:
                        act.wait_ge(oh_used, sum(GROUPS[:gr + 1]))
                    if gr >= 1 and jb == 0:
                        act.wait_ge(packed_used, gr)
                    act.activation(packed[:, jb, :], y_ps[0:TB, jb, 0:OW], ACT.Copy).then_inc(packed_ready, 1)

            counts_to_int(0)
            transposed_hi(0)
            for b in range(NB):
                act.wait_ge(h32_ready, b + 1)
                act.activation(hg_hi[:, b, :], h32[:, b % 2, :], ACT.Copy).then_inc(hg_hi_ready, 1)
            act.wait_ge(w_in[0], 32)
            for m in range(PIECES):
                act.activation(w_hi[0][:, m, :], w_raw[0][:, m, :], ACT.Copy).then_inc(w_hi_ready, 1)
            act.wait_ge(ffn_vec_in, 64)
            act.activation(rwt_hi[:], rwt[:], ACT.Copy).then_inc(rt_hi_ready, 1)
            counts_to_int(1)
            counts_to_int(2)
            act.wait_ge(sbc_done, 1)
            act.activation(s_bc[:, 0:4 * TB], r_ps[0:TB, 1, 0:4 * TB], ACT.Copy).then_inc(sbc_copied, 1)
            act.activation(s_bc[:, 4 * TB:N], r_ps[0:TB, 2, 0:TB], ACT.Copy).then_inc(sbc_copied, 1)
            act.wait_ge(sbc_copied, 2)
            for jb in range(NB):
                if jb >= 2:
                    act.wait_ge(attn_ready, jb - 1)
                act.activation(ex[:, jb % 2, 0, :], s_bc[:], ACT.Exp, bias=s_src_b[:, jb:jb + 1]).then_inc(ex_ready, 1)
                act.activation(ex[:, jb % 2, 1, :], s_bc[:], ACT.Exp, bias=s_src_s[:, jb:jb + 1],
                               scale=SLOPE).then_inc(ex_ready, 1)
                if jb >= 1:
                    act.wait_ge(attn_ready, jb)
                    act.activation(attn_hi[:, jb - 1, :], count[:, jb - 1, :], ACT.Copy).then_inc(attn_hi_ready, 1)
            act.wait_ge(attn_ready, NB)
            act.activation(attn_hi[:, NB - 1, :], count[:, NB - 1, :], ACT.Copy).then_inc(attn_hi_ready, 1)
            transposed_hi(NB)
            act.wait_ge(logits_ready, 1)
            act.activation(e_neg[:], logits[:], ACT.Exp, scale=-1.0).then_inc(e_neg_ready, 1)

            def expert(e, last):
                act.wait_ge(b1_ready, e + 1)
                for c in range(CH):
                    for t in range(TC):
                        j = TC * c + t
                        for hf, (n0, nw) in enumerate(HALVES):
                            u = 2 * j + hf
                            act.wait_ge(h_done, e * UNITS + u + 1)
                            if j >= 2:
                                act.wait_ge(h_ready, e * UNITS + u - 3)
                            act.activation(g[:, j % 2, n0:n0 + nw], r_ps[:, u % 3, 0:nw], ACT.Gelu,
                                           bias=b1_now[:, j:j + 1]).then_inc(gelu_done, 1)
                        if last and c == CH - 1:
                            continue
                        for m in (2 * t, 2 * t + 1):
                            s = (c + 1) % 2
                            if m == 0:
                                act.wait_ge(w_in[s], e * (32 * CH // 2) + 32 * ((c + 1) // 2 + 1))
                            if c == CH - 1 and m == PIECES - 1:
                                act.wait_ge(gelu_done, e * UNITS + UNITS)
                            act.activation(w_hi[s][:, m, :], w_raw[s][:, m, :], ACT.Copy).then_inc(w_hi_ready, 1)
                if not last:
                    act.activation(b1_now[:], b1_sb[:, bass.ds(e * HT + HT, HT)], ACT.Copy).then_inc(b1_ready, 1)

            act.activation(b1_now[:], b1_sb[:, 0:HT], ACT.Copy).then_inc(b1_ready, 1)
            with act.Fori(0, E - 1) as e:
                expert(e, False)
            expert(E - 1, True)

        @block.vector
        def _(dve):
            seq = [0]

            def landed():
                seq[0] += 1
                return seq[0]

            def layernorm_stats(b):
                dve.bn_stats(stats[:, b, :], acc[:, b, :]).then_inc(dve_seq, 1)
                dve.wait_ge(dve_seq, landed())
                dve.bn_aggr(moments[:, b, :], stats[:, b, :]).then_inc(dve_seq, 1)
                dve.wait_ge(dve_seq, landed())

            def layernorm_apply(b):
                dve.tensor_scalar(xn[:, b, :], acc[:, b, :], moments[:, b, 0:1], rstd[:, b:b + 1],
                                  ALU.subtract, ALU.mult).then_inc(xn_ready, 1)

            def transposed_lo(i):
                b = i % NB
                dve.wait_ge(xt_hi_ready, i + 1)
                dve.tensor_tensor(xt_lo[:, :, b * TB:(b + 1) * TB],
                                  r_ps[:, TP_BANK[i], 0:DK * TB].rearrange("p (k n) -> p k n", k=DK),
                                  xt_hi[:, :, b * TB:(b + 1) * TB].bitcast(F32), ALU.subtract).then_inc(xt_ready, 1)

            def by_step(ap):
                return ap.rearrange("p (i s) -> p i s", s=OH_SLOTS)

            def one_hot_step(i, wait_free):
                for s in range(OH_SLOTS):
                    if wait_free:
                        dve.wait_ge(oh_used, i * OH_SLOTS + s - (OH_SLOTS - 1))
                    col = bass.ds(i, 1)
                    dve.tensor_scalar(oh_src[:, s, :], iota_src[:], by_step(edge_f[:, 0, :])[:, col, s], None,
                                      ALU.is_equal)
                    dve.tensor_scalar(oh_dst[:, s, :], iota_src[:, 0:OW], by_step(dst_lo[:])[:, col, s],
                                      by_step(dst_val[:])[:, col, s],
                                      ALU.is_equal, ALU.mult).then_inc(oh_ready, 1)

            def one_hots(gr):
                first = sum(GROUPS[:gr]) // OH_SLOTS
                if gr == 0:
                    one_hot_step(0, False)
                    first = 1
                with dve.Fori(first, sum(GROUPS[:gr + 1]) // OH_SLOTS) as i:
                    one_hot_step(i, True)

            def decode(gr):
                dve.wait_ge(packed_ready, NB * (gr + 1))
                dve.tensor_scalar(cnt_up[:], packed[:], FIELD_BITS, None, ALU.logical_shift_right).then_inc(dve_seq, 1)
                landed()
                dve.tensor_scalar(cnt_dn[:], packed[:], int(FIELD) - 1, None, ALU.bitwise_and).then_inc(packed_used, 1)
                dve.wait_ge(dve_seq, seq[0])
                dve.wait_ge(packed_used, gr + 1)
                for field, a, b in ((cnt_up, LO_N, N), (cnt_dn, 0, LO_N)):
                    if gr == 0:
                        i = dve.tensor_copy(count[:, :, a:b], field[:, :, 0:b - a])
                    else:
                        i = dve.tensor_tensor(count[:, :, a:b], count[:, :, a:b], field[:, :, 0:b - a], ALU.add)
                    i.then_inc(dve_seq, 1)
                    landed()
                dve.wait_ge(dve_seq, seq[0])

            dve.wait_ge(edges_in, 32)
            dve.tensor_copy(edge_f[:], edge_i[:]).then_inc(dve_seq, 1)
            dve.wait_ge(dve_seq, landed())
            dve.tensor_scalar(upper[:], edge_f[:, 1, :], float(LO_N), None, ALU.is_ge).then_inc(dve_seq, 1)
            dve.wait_ge(dve_seq, landed())
            dve.scalar_tensor_tensor(dst_lo[:], upper[:], -float(LO_N), edge_f[:, 1, :], ALU.mult,
                                     ALU.add).then_inc(dve_seq, 1)
            landed()
            dve.tensor_scalar(dst_val[:], upper[:], FIELD - 1.0, 1.0, ALU.mult, ALU.add).then_inc(dve_seq, 1)
            dve.wait_ge(dve_seq, landed())
            dve.wait_ge(iota_ready, 1)
            dve.wait_ge(consts_ready, CONSTS)
            one_hots(0)

            dve.wait_ge(x_in, 16)
            for b in range(NB):
                layernorm_stats(b)
            dve.tensor_scalar(var_eps[:], moments[:, :, 1], EPS, None, ALU.add).then_inc(ve_ready, 1)
            for k in range(DK):
                dve.wait_ge(wg_hi_ready, k + 1)
                dve.tensor_tensor(wg_lo[:, k, :], wg_raw[:, k, :], wg_hi[:, k, :].bitcast(F32),
                                  ALU.subtract).then_inc(wg_ready, 1)
            dve.wait_ge(rstd_ready, 1)
            for b in range(NB):
                layernorm_apply(b)
            for b in range(NB):
                transposed_lo(b)
            decode(0)
            dve.wait_ge(vec_in, 64)
            for b in range(NB):
                dve.wait_ge(hg_done, b + 1)
                dve.tensor_tensor(h32[:, b % 2, :], r_ps[0:TB, (b + 2) % 3, :], bw_bc[:], ALU.add).then_inc(h32_ready, 1)
                dve.wait_ge(h32_ready, b + 1)
                for s, half in ((s_dst, 0), (s_src, 1)):
                    dve.tensor_tensor_reduce(out=scratch[:], in0=h32[:, b % 2, :], in1=a_bc[:, half, :], scale=1.0,
                                             scalar=0.0, op0=ALU.mult, op1=ALU.add,
                                             accum_out=s[:, b:b + 1]).then_inc(dve_seq, 1)
                    dve.wait_ge(dve_seq, landed())
                dve.wait_ge(hg_hi_ready, b + 1)
                dve.tensor_tensor(hg_lo[:, b, :], h32[:, b % 2, :], hg_hi[:, b, :].bitcast(F32),
                                  ALU.subtract).then_inc(hg_ready, 1)
            dve.tensor_scalar(s_src_b[:], s_src[:], ba_bc[:, 0:1], None, ALU.add).then_inc(dve_seq, 1)
            dve.wait_ge(dve_seq, landed())
            dve.tensor_scalar(s_src_s[:], s_src_b[:], SLOPE, None, ALU.mult).then_inc(dve_seq, 1)
            dve.wait_ge(dve_seq, landed())
            one_hots(1)
            decode(1)
            one_hots(2)
            dve.wait_ge(oh_used, EC)
            decode(2)
            for b in range(NB):
                dve.tensor_scalar(diag[:, b, :], ident[0:TB, 0:TB], s_dst[:, b:b + 1], None,
                                  ALU.mult).then_inc(diag_ready, 1)
            for m in range(PIECES):
                dve.wait_ge(w_hi_ready, m + 1)
                dve.tensor_tensor(w_lo[0][:, m, :], w_raw[0][:, m, :], w_hi[0][:, m, :].bitcast(F32),
                                  ALU.subtract).then_inc(w_ready, 1)
            dve.wait_ge(rt_hi_ready, 1)
            dve.tensor_tensor(rwt_lo[:], rwt[:], rwt_hi[:].bitcast(F32), ALU.subtract).then_inc(rt_ready, 1)
            for jb in range(NB + 1):
                if jb < NB:
                    dve.wait_ge(ex_ready, 2 * jb + 2)
                    dve.tensor_tensor(ex[:, jb % 2, 0, :], ex[:, jb % 2, 0, :], ex[:, jb % 2, 1, :],
                                      ALU.max).then_inc(ex_max, 1)
                    dve.wait_ge(ex_max, jb + 1)
                    dve.scalar_tensor_tensor(count[:, jb, :], ex[:, jb % 2, 0, :], FLT_MAX, count[:, jb, :],
                                             ALU.min, ALU.mult).then_inc(attn_ready, 1)
                if jb >= 1:
                    dve.wait_ge(attn_hi_ready, jb)
                    dve.tensor_tensor(attn_lo[:, jb - 1, :], count[:, jb - 1, :],
                                      attn_hi[:, jb - 1, :].bitcast(F32), ALU.subtract).then_inc(attn_lo_ready, 1)
            for b in range(NB + 1):
                if b < NB:
                    dve.wait_ge(den_done, b + 1)
                    dve.tensor_copy(den[:, b:b + 1], r_ps[0:TB, DEN_BANK[b], 0:1]).then_inc(dve_seq, 1)
                    dve.wait_ge(dve_seq, landed())
                    dve.tensor_scalar(den_zero[:, b:b + 1], den[:, b:b + 1], 0.0, None,
                                      ALU.is_equal).then_inc(dve_seq, 1)
                    dve.wait_ge(dve_seq, landed())
                    dve.tensor_tensor(den_safe[:, b:b + 1], den[:, b:b + 1], den_zero[:, b:b + 1],
                                      ALU.add).then_inc(dve_seq, 1)
                    dve.wait_ge(dve_seq, landed())
                    dve.reciprocal(rden[:, b:b + 1], den_safe[:, b:b + 1]).then_inc(den_read, 1)
                    dve.wait_ge(den_read, b + 1)
                    dve.wait_ge(agg_done, b + 1)
                    dve.scalar_tensor_tensor(acc[:, b, :], y_ps[0:TB, b, :], rden[:, b:b + 1], acc[:, b, :],
                                             ALU.mult, ALU.add).then_inc(y_added, 1)
                    dve.wait_ge(y_added, b + 1)
                    layernorm_stats(b)
                    dve.tensor_scalar(var_eps[:, b:b + 1], moments[:, b, 1:2], EPS, None, ALU.add).then_inc(ve_ready, 1)
                if b >= 1:
                    dve.wait_ge(rstd_ready, 1 + b)
                    layernorm_apply(b - 1)
            for b in range(NB):
                transposed_lo(NB + b)
            dve.wait_ge(router_done, 1)
            for b in range(NB):
                i = dve.tensor_tensor(logits[:, b, :], r_ps[0:TB, 1, 8 * b:8 * b + 7], rb_bc[:], ALU.add)
            i.then_inc(logits_ready, 1)
            dve.wait_ge(e_neg_ready, 1)
            dve.tensor_scalar(e_neg[:], e_neg[:], 1.0, None, ALU.add).then_inc(dve_seq, 1)
            dve.wait_ge(dve_seq, landed())
            dve.reciprocal(prob[:, :, :, 1], e_neg[:]).then_inc(dve_seq, 1)
            dve.wait_ge(dve_seq, landed())
            dve.tensor_scalar(prob[:, :, :, 0], prob[:, :, :, 1], -1.0, 1.0, ALU.mult, ALU.add).then_inc(dve_seq, 1)
            dve.wait_ge(dve_seq, landed())
            for m in range(4):
                dve.tensor_tensor(pair[:, :, m], prob[:, :, 0, m // 2], prob[:, :, 1 + m // 2, m % 2],
                                  ALU.mult).then_inc(dve_seq, 1)
                landed()
            dve.wait_ge(dve_seq, seq[0])
            for n in range(E):
                dve.tensor_tensor(leaf[:, :, n], pair[:, :, n // 2], prob[:, :, 3 + n // 2, n % 2],
                                  ALU.mult).then_inc(dve_seq, 1)
                landed()
            dve.wait_ge(dve_seq, seq[0])

            def expert(e, last):
                for c in range(CH):
                    for t in range(TC):
                        j = TC * c + t
                        for hf, (n0, nw) in enumerate(HALVES):
                            u = 2 * j + hf
                            cols = slice(n0, n0 + nw)
                            dve.wait_ge(gelu_done, e * UNITS + u + 1)
                            if hf == 0 and j >= 2:
                                dve.wait_ge(l2_done, e * (HT - 1) + j - 1)
                            dve.tensor_copy(h_hi[:, j % 2, cols], g[:, j % 2, cols]).then_inc(h_hi_ready, 1)
                            dve.wait_ge(h_hi_ready, e * UNITS + u + 1)
                            dve.tensor_tensor(h_lo[:, j % 2, cols], g[:, j % 2, cols],
                                              h_hi[:, j % 2, cols].bitcast(F32), ALU.subtract).then_inc(h_ready, 1)
                        if 2 <= j < 2 + NB:
                            b = j - 2
                            if b == 0:
                                dve.wait_ge(y_added, e * NB + NB)
                            dve.scalar_tensor_tensor(acc[:, b, :], b2_bc[:, bass.ds(e, 1), :].rearrange("p e d -> p (e d)"),
                                                     leaf[:, b, bass.ds(e, 1)], acc[:, b, :],
                                                     ALU.mult, ALU.add).then_inc(b2_added, 1)
                        if last and c == CH - 1:
                            continue
                        for m in (2 * t, 2 * t + 1):
                            s = (c + 1) % 2
                            dve.wait_ge(w_hi_ready, e * (CH * PIECES) + PIECES * (c + 1) + m + 1)
                            dve.tensor_tensor(w_lo[s][:, m, :], w_raw[s][:, m, :], w_hi[s][:, m, :].bitcast(F32),
                                              ALU.subtract).then_inc(w_ready, 1)
                dve.wait_ge(b2_added, e * NB + NB)
                for b in range(NB):
                    dve.wait_ge(y_done, e * NB + b + 1)
                    dve.scalar_tensor_tensor(acc[:, b, :], y_ps[0:TB, b, :], leaf[:, b, bass.ds(e, 1)], acc[:, b, :],
                                             ALU.mult, ALU.add).then_inc(y_added, 1)

            with dve.Fori(0, E - 1) as e:
                expert(e, False)
            expert(E - 1, True)

        @block.tensor
        def _(pe):
            def product(out_ap, lhs, rhs, start, stop):
                pe.matmul(out_ap, lhs[0], rhs[0], start=start, stop=False)
                pe.matmul(out_ap, lhs[0], rhs[1], start=False, stop=False)
                return pe.matmul(out_ap, lhs[1], rhs[0], start=False, stop=stop)

            def transpose_block(i):
                b = i % NB
                pe.wait_ge(xn_ready, i + 1)
                for k in range(DK):
                    m = pe.transpose(r_ps[:, TP_BANK[i], k * TB:(k + 1) * TB], xn[:, b, k * P:(k + 1) * P],
                                     ident[0:TB, 0:TB])
                m.then_inc(tp_done, 1)

            def count_step(c0, gr, first, last):
                for s in range(OH_SLOTS):
                    pe.wait_ge(oh_ready, c0 + s + 1)
                    for jb in range(NB):
                        if gr >= 1 and first and s == 0:
                            pe.wait_ge(packed_ready, NB * (gr - 1) + jb + 1)
                        m = pe.matmul(y_ps[0:TB, jb, 0:OW], oh_src[:, s, jb * TB:(jb + 1) * TB], oh_dst[:, s, :],
                                      start=first and s == 0, stop=last and s == OH_SLOTS - 1)
                        if last and s == OH_SLOTS - 1 and jb < NB - 1:
                            m.then_inc(cnt_done, 1)
                    m.then_inc(oh_used, 1)

            def counts(gr):
                a, b = sum(GROUPS[:gr]), sum(GROUPS[:gr + 1])
                count_step(a, gr, True, False)
                with pe.Fori(a + OH_SLOTS, b - OH_SLOTS, OH_SLOTS) as c0:
                    count_step(c0, gr, False, False)
                count_step(b - OH_SLOTS, gr, False, True)

            pe.wait_ge(consts_ready, CONSTS)
            counts(0)
            for b in range(NB):
                if b >= 3:
                    pe.wait_ge(xt_ready, b - 2)
                transpose_block(b)
            pe.wait_ge(wg_ready, DK)
            for b in range(NB):
                if b < 3:
                    pe.wait_ge(xt_ready, b + 3)
                else:
                    pe.wait_ge(h32_ready, b - 2)
                for k in range(DK):
                    cols = slice(b * TB, (b + 1) * TB)
                    m = product(r_ps[0:TB, (b + 2) % 3, :], (xt_hi[:, k, cols], xt_lo[:, k, cols]),
                                (wg_hi[:, k, :], wg_lo[:, k, :]), k == 0, k == DK - 1)
                m.then_inc(hg_done, 1)
            counts(1)
            counts(2)
            pe.wait_ge(h32_ready, NB)
            for b in range(NB):
                pe.wait_ge(diag_ready, b + 1)
                m = pe.matmul(r_ps[0:TB, 1 + b // 4, (b % 4) * TB:(b % 4 + 1) * TB], ones_f[:], diag[:, b, :],
                              start=True, stop=True)
            m.then_inc(sbc_done, 1)

            def attend(ib, jb):
                cols = slice(ib * TB, (ib + 1) * TB)
                return product(y_ps[0:TB, ib, :], (attn_hi[:, jb, cols], attn_lo[:, jb, cols]),
                               (hg_hi[:, jb, :], hg_lo[:, jb, :]), jb == 0, jb == NB - 1)

            def denominator(ib):
                if ib >= 3:
                    pe.wait_ge(den_read, ib - 2)
                for jb in range(NB):
                    for n, part in enumerate((attn_hi, attn_lo)):
                        m = pe.matmul(r_ps[0:TB, DEN_BANK[ib], 0:2], part[:, jb, ib * TB:(ib + 1) * TB], ones_r[:],
                                      start=jb == 0 and n == 0, stop=jb == NB - 1 and n == 1)
                m.then_inc(den_done, 1)

            pe.wait_ge(packed_ready, NB * len(GROUPS))
            pe.wait_ge(hg_ready, NB)
            pe.wait_ge(sbc_copied, 2)
            for jb in range(NB):
                pe.wait_ge(attn_lo_ready, jb + 1)
                for ib in (0, 1):
                    m = attend(ib, jb)
                    if jb == NB - 1:
                        m.then_inc(agg_done, 1)
            denominator(0)
            denominator(1)
            for ib in range(2, NB):
                for jb in range(NB):
                    m = attend(ib, jb)
                m.then_inc(agg_done, 1)
                denominator(ib)
                if ib == 3:
                    pe.wait_ge(den_read, 3)
                    transpose_block(NB)
            pe.wait_ge(den_read, 4)
            transpose_block(NB + 1)
            pe.wait_ge(den_read, 5)
            transpose_block(NB + 2)
            for b in (3, 4):
                pe.wait_ge(xt_ready, NB + b - 2)
                transpose_block(NB + b)
            pe.wait_ge(rt_ready, 1)
            pe.wait_ge(xt_ready, NB + 3)
            for b in range(NB):
                pe.wait_ge(xt_ready, NB + b + 1)
                for k in range(DK):
                    cols = slice(b * TB, (b + 1) * TB)
                    m = product(r_ps[0:TB, 1, 8 * b:8 * b + 8], (xt_hi[:, k, cols], xt_lo[:, k, cols]),
                                (rwt_hi[:, k, :], rwt_lo[:, k, :]), k == 0, k == DK - 1)
            m.then_inc(router_done, 1)
            pe.wait_ge(logits_ready, 1)

            def hidden(e, j):
                s, t = (j // TC) % 2, j % TC
                if t == 0:
                    pe.wait_ge(w_ready, e * (CH * PIECES) + PIECES * (j // TC) + DK)
                for hf, (n0, nw) in enumerate(HALVES):
                    u = 2 * j + hf
                    if u >= 3:
                        pe.wait_ge(gelu_done, e * UNITS + u - 2)
                    for k in range(DK):
                        cols = slice(n0, n0 + nw)
                        wc = slice(t * P, (t + 1) * P)
                        m = product(r_ps[:, u % 3, 0:nw], (w_hi[s][:, k, wc], w_lo[s][:, k, wc]),
                                    (xt_hi[:, k, cols], xt_lo[:, k, cols]), k == 0, k == DK - 1)
                    m.then_inc(h_done, 1)

            def output(e, j):
                s, t = (j // TC) % 2, j % TC
                pe.wait_ge(w_ready, e * (CH * PIECES) + PIECES * (j // TC) + DK + t + 1)
                pe.wait_ge(h_ready, e * UNITS + 2 * j + 2)
                if j == 0:
                    pe.wait_ge(y_added, e * NB + NB)
                for b in range(NB):
                    cols = slice(b * TB, (b + 1) * TB)
                    m = product(y_ps[0:TB, b, :], (h_hi[:, j % 2, cols], h_lo[:, j % 2, cols]),
                                (w_hi[s][:, DK + t, :], w_lo[s][:, DK + t, :]), j == 0, j == HT - 1)
                    if j == HT - 1:
                        m.then_inc(y_done, 1)
                if j < HT - 1:
                    m.then_inc(l2_done, 1)

            with pe.Fori(0, E) as e:
                hidden(e, 0)
                for j in range(1, HT):
                    hidden(e, j)
                    output(e, j - 1)
                output(e, HT - 1)


TP_BANK = (0, 1, 2, 0, 1, 2, 0, 1, 2, 0)
DEN_BANK = (0, 1, 2, 0, 1)


def kernel(x, src, dst, L0_gnn_W, L0_gnn_b_w, L0_gnn_a, L0_gnn_b_a, L0_ffn_rw, L0_ffn_rb, L0_ffn_w1, L0_ffn_b1,
           L0_ffn_w2, L0_ffn_b2):
    import numpy as np
    import concourse.bacc as bacc
    from concourse.bass_utils import run_bass_kernel_spmd

    rw = np.asarray(L0_ffn_rw)
    rw_t = rw.reshape(rw.shape[0], DK, P).transpose(2, 1, 0).reshape(P, -1)
    b1_t = np.asarray(L0_ffn_b1).reshape(E * HT, P).T
    ins = {
        "x": x, "src": src, "dst": dst, "w_gnn": L0_gnn_W, "b_w": L0_gnn_b_w, "a_vec": L0_gnn_a,
        "b_a": np.asarray(L0_gnn_b_a).reshape(1), "rw_t": rw_t, "rb": L0_ffn_rb, "w1": L0_ffn_w1, "b1_t": b1_t,
        "w2": L0_ffn_w2, "b2": L0_ffn_b2,
    }
    nc = bacc.Bacc("TRN2", target_bir_lowering=False, num_devices=1)
    arrays, args = {}, {}
    for name, value in ins.items():
        value = np.ascontiguousarray(value)
        arrays[f"in_{name}"] = value
        args[name] = nc.dram_tensor(f"in_{name}", value.shape, mybir.dt.from_np(value.dtype), kind="ExternalInput").ap()
    args["out"] = nc.dram_tensor("out_x", (N, D), F32, kind="ExternalOutput").ap()
    gnn_ffn_kernel(nc, **args)
    result = run_bass_kernel_spmd(nc, [arrays], core_ids=[0])
    return result.results[0]["out_x"]
```

```python
from contextlib import ExitStack

import concourse.bass as bass
from concourse import mybir

ALU = mybir.AluOpType
ACT = mybir.ActivationFunctionType
F32 = mybir.dt.float32
F32R = mybir.dt.float32r
F16 = mybir.dt.float16
I32 = mybir.dt.int32

P = 128
N = 625
TB = 125
NB = N // TB
D = 512
DK = D // P
E = 8
HID = 2048
HT = HID // P
CW = 512
CH = HID // CW
TC = CW // P
NP = N + 1
HALVES = ((0, 314), (314, 312))
ROUND_DOWN = 0.4375
UNITS = 2 * HT
PIECES = DK + TC
EPS = 1e-5
SLOPE = 0.2
FLT_MAX = 3.4028234663852886e38

EDGES = 10000
EC = EDGES // TB
LO_N = 313
OW = 314
SW = 626
FIELD = 4096.0
FIELD_BITS = 12
STEP = 4
OH_STEPS = 3
GROUPS = (7, 7, 6)
ACT_ROWS = (1, 1, 2, 2) + (1,) * 16
CONSTS = 8
assert sum(GROUPS) * STEP == EC and max(GROUPS) * STEP * TB < FIELD



def gnn_ffn_kernel(nc, x, src, dst, w_gnn, b_w, a_vec, b_a, rw_t, rb, w1, b1_t, w2, b2, out):
    with ExitStack() as ctx:
        def sb(scope, name, shape, dt=F32):
            return scope.enter_context(nc.sbuf_tensor(name, shape, dt))

        def sem(name):
            return ctx.enter_context(nc.semaphore(name))

        y_ps = ctx.enter_context(nc.psum_tensor("y_ps", [P, NB, 512], F32))
        r_ps = ctx.enter_context(nc.psum_tensor("r_ps", [P, 3, 512], F32))

        acc = sb(ctx, "acc", [TB, NB, D])
        xn = sb(ctx, "xn", [TB, NB, D])
        xt_hi = sb(ctx, "xt_hi", [P, DK, NP], F32R)
        xt_lo = sb(ctx, "xt_lo", [P, DK, NP], F32R)
        ident = sb(ctx, "ident", [P, P])
        stats = sb(ctx, "stats", [TB, NB, 6])
        moments = sb(ctx, "moments", [TB, NB, 2])
        var_eps = sb(ctx, "var_eps", [TB, NB])
        minus_half = sb(ctx, "minus_half", [TB, NB])
        rstd = sb(ctx, "rstd", [TB, NB])
        leaf = sb(ctx, "leaf", [TB, NB, E])
        rb_col = sb(ctx, "rb_col", [7, 1])
        rb_neg = sb(ctx, "rb_neg", [7, 1])
        e_neg_t = sb(ctx, "e_neg_t", [7, NP])
        one_plus = sb(ctx, "one_plus", [TB, NB, 7])
        prob = sb(ctx, "prob", [TB, NB, 7, 2])
        pair = sb(ctx, "pair", [TB, NB, 4])
        b1_sb = sb(ctx, "b1_sb", [P, E * HT])
        b1_now = sb(ctx, "b1_now", [P, HT])
        w_raw = [sb(ctx, "w_raw0", [P, PIECES, CW])]
        w_hi = [sb(ctx, "w_hi0", [P, PIECES, CW], F32R)]
        w_lo = [sb(ctx, "w_lo0", [P, PIECES, CW], F32R)]

        with ExitStack() as gnn:
            wg_raw = w_raw[0][:, 0:DK, :]
            count = sb(gnn, "count", [TB, NB, 2, OW], I32)
            hg_hi = sb(gnn, "hg_hi", [TB, NB, D], F32R)
            hg_lo = sb(gnn, "hg_lo", [TB, NB, D], F32R)
            h = xn[:, 0:2, :]
            a_bc = xn[:, 2:4, :]
            bw_bc = xn[:, 4, :]
            rwt = sb(gnn, "rwt", [P, DK, P])
            rwt_hi = sb(gnn, "rwt_hi", [P, DK, P], F32R)
            rwt_lo = sb(gnn, "rwt_lo", [P, DK, P], F32R)
            ba_bc = sb(gnn, "ba_bc", [TB, 1])
            s_dst = sb(gnn, "s_dst", [TB, NB])
            s_src = sb(gnn, "s_src", [TB, NB])
            s_src_b = sb(gnn, "s_src_b", [TB, NB])
            s_src_s = sb(gnn, "s_src_s", [TB, NB])
            s_bc = sb(gnn, "s_bc", [TB, NP])
            ex_lin = sb(gnn, "ex_lin", [TB, NB, NP])
            ex_sl = sb(gnn, "ex_sl", [TB, 2, NP])
            scratch = ex_sl[:, 0, 0:D]
            diag = ex_sl[:, 1, 0:N].rearrange("p (b n) -> p b n", b=NB)
            ones_f = sb(gnn, "ones_f", [TB, TB])
            iota_src = sb(gnn, "iota_src", [TB, SW], F16)
            edge_i = sb(gnn, "edge_i", [TB, 2, EC], I32)
            edge_f = sb(gnn, "edge_f", [TB, 2, EC])
            upper = sb(gnn, "upper", [TB, EC])
            dst_lo = sb(gnn, "dst_lo", [TB, EC])
            dst_val = sb(gnn, "dst_val", [TB, EC])
            dst_lo_neg = sb(gnn, "dst_lo_neg", [TB, EC])
            dst_val_neg = sb(gnn, "dst_val_neg", [TB, EC])
            distance = sb(gnn, "distance", [TB, 2, OW], F16)
            shift = sb(gnn, "shift", [TB, NB])
            count_up = sb(gnn, "count_up", [TB, NB, OW], I32)
            count_dn = sb(gnn, "count_dn", [TB, NB, OW], I32)
            den = sb(gnn, "den", [TB, NB])
            den_safe = sb(gnn, "den_safe", [TB, NB])
            rden = sb(gnn, "rden", [TB, NB])
            with ExitStack() as early:
                wg_hi = sb(early, "wg_hi", [P, DK, D], F32R)
                wg_lo = sb(early, "wg_lo", [P, DK, D], F32R)
                oh_src = sb(early, "oh_src", [TB, OH_STEPS * STEP, SW], F16)
                oh_dst = sb(early, "oh_dst", [TB, OH_STEPS * STEP, OW], F16)
            with ExitStack() as late:
                attn_hi = sb(late, "attn_hi", [TB, NB, NP], F32R)
                attn_lo = sb(late, "attn_lo", [TB, NB, NP], F32R)
        w_raw.append(sb(ctx, "w_raw1", [P, PIECES, CW]))
        w_hi.append(sb(ctx, "w_hi1", [P, PIECES, CW], F32R))
        w_lo.append(sb(ctx, "w_lo1", [P, PIECES, CW], F32R))
        b2_bc = sb(ctx, "b2_bc", [TB, E, D])
        g = sb(ctx, "g", [P, 2, NP])
        h_hi = sb(ctx, "h_hi", [P, 2, NP], F32R)
        h_lo = sb(ctx, "h_lo", [P, 2, NP], F32R)

        x_in = sem("x_in")
        edges_in = sem("edges_in")
        wg_in = sem("wg_in")
        vec_in = sem("vec_in")
        ffn_vec_in = sem("ffn_vec_in")
        b2_in = sem("b2_in")
        w_in = [sem("w_in0"), sem("w_in1")]
        out_written = sem("out_written")
        pool_seq = sem("pool_seq")
        consts_ready = sem("consts_ready")
        iota_ready = sem("iota_ready")
        dve_seq = sem("dve_seq")
        ve_ready = sem("ve_ready")
        rstd_ready = sem("rstd_ready")
        xn_ready = sem("xn_ready")
        tp_done = sem("tp_done")
        xt_hi_ready = sem("xt_hi_ready")
        xt_ready = sem("xt_ready")
        wg_hi_ready = sem("wg_hi_ready")
        wg_ready = sem("wg_ready")
        hg_done = sem("hg_done")
        oh_ready = sem("oh_ready")
        oh_far_ready = sem("oh_far_ready")
        distance_ready = sem("distance_ready")
        oh_used = sem("oh_used")
        count_up_ready = sem("count_up_ready")
        up_added = sem("up_added")
        dn_added = sem("dn_added")
        keys_ready = sem("keys_ready")
        counts_read = sem("counts_read")
        shift_ready = sem("shift_ready")
        hg_ready = sem("hg_ready")
        hg_hi_ready = sem("hg_hi_ready")
        hg_lo_ready = sem("hg_lo_ready")
        rb_ready = sem("rb_ready")
        tree_done = sem("tree_done")
        tree_read = sem("tree_read")
        cnt_done = sem("cnt_done")
        scores_ready = sem("scores_ready")
        diag_ready = sem("diag_ready")
        sbc_done = sem("sbc_done")
        sbc_copied = sem("sbc_copied")
        ex_max = sem("ex_max")
        ex_ready = sem("ex_ready")
        attn_ready = sem("attn_ready")
        attn_hi_ready = sem("attn_hi_ready")
        attn_lo_ready = sem("attn_lo_ready")
        agg_done = sem("agg_done")
        den_done = sem("den_done")
        den_read = sem("den_read")
        rt_hi_ready = sem("rt_hi_ready")
        rt_ready = sem("rt_ready")
        router_done = sem("router_done")
        e_neg_ready = sem("e_neg_ready")
        w_hi_ready = sem("w_hi_ready")
        w_ready = sem("w_ready")
        b1_ready = sem("b1_ready")
        h_done = sem("h_done")
        gelu_done = sem("gelu_done")
        h_hi_ready = sem("h_hi_ready")
        h_ready = sem("h_ready")
        l2_done = sem("l2_done")
        y_done = sem("y_done")
        y_added = sem("y_added")
        b2_added = sem("b2_added")

        w1_v = w1.rearrange("e (k p) n -> e p k n", p=P)
        w2_v = w2.rearrange("e (t p) n -> e p t n", p=P)

        block = ctx.enter_context(nc.Block())

        @block.sync
        def _(sp):
            sp.dma_start(edge_i[:, 0, :], src.rearrange("(p c) -> p c", c=EC)).then_inc(edges_in, 16)
            sp.dma_start(edge_i[:, 1, :], dst.rearrange("(p c) -> p c", c=EC)).then_inc(edges_in, 16)
            sp.dma_start(acc[:], x.rearrange("(b p) d -> p b d", p=TB)).then_inc(x_in, 16)
            sp.dma_start(wg_raw, w_gnn.rearrange("(k p) n -> p k n", p=P)).then_inc(wg_in, 16)
            def load_chunk(e, c):
                slot = c % 2
                sp.dma_start(w_raw[slot][:, 0:DK, :], w1_v[bass.ds(e, 1), :, :, c * CW:(c + 1) * CW]
                             .rearrange("e p k n -> p (e k) n")).then_inc(w_in[slot], 16)
                sp.dma_start(w_raw[slot][:, DK:PIECES, :], w2_v[bass.ds(e, 1), :, c * TC:(c + 1) * TC, :]
                             .rearrange("e p t n -> p (e t) n")).then_inc(w_in[slot], 16)

            sp.wait_ge(tp_done, NB)
            sp.dma_start(bw_bc[:], b_w.partition_broadcast(TB)).then_inc(vec_in, 16)
            sp.dma_start(a_bc[:, 0, :], a_vec[0:D].partition_broadcast(TB)).then_inc(vec_in, 16)
            sp.dma_start(a_bc[:, 1, :], a_vec[D:2 * D].partition_broadcast(TB)).then_inc(vec_in, 16)
            sp.dma_start(ba_bc[:], b_a.partition_broadcast(TB)).then_inc(vec_in, 16)
            sp.wait_ge(wg_ready, DK)
            load_chunk(0, 0)
            sp.wait_ge(consts_ready, CONSTS)
            sp.dma_start(rwt[:, :, 0:7], rw_t.rearrange("p (k n) -> p k n", k=DK)).then_inc(ffn_vec_in, 16)
            sp.dma_start(rb_col[:], rb.rearrange("(p n) -> p n", n=1)).then_inc(ffn_vec_in, 16)
            sp.dma_start(b1_sb[:], b1_t).then_inc(ffn_vec_in, 16)
            sp.wait_ge(agg_done, NB)
            sp.wait_ge(den_done, NB)
            sp.wait_ge(router_done, 2)
            load_chunk(0, 1)
            sp.dma_start(b2_bc[:].rearrange("p e d -> p (e d)"),
                         b2.rearrange("e d -> (e d)").partition_broadcast(TB)).then_inc(b2_in, 16)
            for c in (2, 3):
                sp.wait_ge(w_ready, PIECES * (c - 1))
                load_chunk(0, c)
            with sp.Fori(1, E) as e:
                for c in range(CH):
                    sp.wait_ge(w_ready, e * (CH * PIECES) + PIECES * (c - 1))
                    load_chunk(e, c)
            for b in range(NB):
                sp.wait_ge(y_added, NB * E + b + 1)
                sp.dma_start(out[b * TB:(b + 1) * TB, :], acc[:, b, :]).then_inc(out_written, 16)
            sp.wait_ge(out_written, 16 * NB)

        @block.gpsimd
        def _(pool):
            pool.iota(iota_src[:], [[1, SW]], base=0, channel_multiplier=0,
                      allow_small_or_imprecise_dtypes=True).then_inc(iota_ready, 1)
            pool.memset(ident[:], 0.0).then_inc(pool_seq, 1)
            pool.wait_ge(pool_seq, 1)
            pool.affine_select(out=ident[:], in_=ident[:], compare_op=ALU.not_equal, fill=1.0, base=0,
                               pattern=[[-1, P]], channel_multiplier=1).then_inc(consts_ready, 1)
            pool.memset(minus_half[:], -0.5).then_inc(consts_ready, 1)
            pool.memset(ones_f[:], 1.0).then_inc(consts_ready, 1)
            pool.memset(xt_hi[:, :, N:NP].bitcast(F32), 0.0).then_inc(consts_ready, 1)
            pool.memset(xt_lo[:, :, N:NP].bitcast(F32), 0.0).then_inc(consts_ready, 1)
            pool.memset(rwt[:], 0.0).then_inc(consts_ready, 1)
            pool.memset(e_neg_t[:, N:NP], 0.0).then_inc(consts_ready, 1)
            pool.memset(s_bc[:, N:NP], 0.0).then_inc(consts_ready, 1)
            pool.wait_ge(consts_ready, CONSTS)
            pool.wait_ge(ve_ready, 1)
            pool.tensor_tensor(rstd[:], var_eps[:], minus_half[:], ALU.pow).then_inc(rstd_ready, 1)
            for k in range(DK):
                pool.wait_ge(wg_hi_ready, k + 1)
                pool.tensor_tensor(wg_lo[:, k, :], wg_raw[:, k, :], wg_hi[:, k, :].bitcast(F32),
                                   ALU.subtract).then_inc(wg_ready, 1)
            for jb in range(NB):
                pool.wait_ge(count_up_ready, jb + 1)
                pool.tensor_copy(count[:, jb, 1, :], count_up[:, jb, :]).then_inc(up_added, 1)
            def weight_lo(*pieces):
                for m in pieces:
                    pool.wait_ge(w_hi_ready, m + 1)
                    pool.tensor_tensor(w_lo[0][:, m, :], w_raw[0][:, m, :], w_hi[0][:, m, :].bitcast(F32),
                                       ALU.subtract).then_inc(w_ready, 1)

            for b in range(NB):
                pool.wait_ge(hg_hi_ready, b + 1)
                pool.tensor_tensor(hg_lo[:, b, :], h[:, b % 2, :], hg_hi[:, b, :].bitcast(F32),
                                   ALU.subtract).then_inc(hg_lo_ready, 1)
                if b >= 1:
                    weight_lo(2 * b - 2, 2 * b - 1)
            pool.wait_ge(rt_hi_ready, 1)
            pool.tensor_tensor(rwt_lo[:], rwt[:], rwt_hi[:].bitcast(F32), ALU.subtract).then_inc(rt_ready, 1)
            for gr in (1, 2):
                for jb in range(NB):
                    pool.wait_ge(up_added, NB * (gr - 1) + jb + 1)
                    pool.wait_ge(count_up_ready, NB * gr + jb + 1)
                    pool.tensor_tensor(count[:, jb, 1, :], count[:, jb, 1, :], count_up[:, jb, :],
                                       ALU.add).then_inc(up_added, 1)
                    pool.wait_ge(counts_read, NB * gr + jb + 1)
                    if gr == 2:
                        pool.wait_ge(dn_added, jb + 1)
                    pool.tensor_tensor(count[:, jb, 0, :], count[:, jb, 0, :], count_dn[:, jb, :],
                                       ALU.add).then_inc(dn_added, 1)
            for b in range(NB):
                pool.wait_ge(ve_ready, 2 + b)
                pool.tensor_tensor(rstd[:, b:b + 1], var_eps[:, b:b + 1], minus_half[:, b:b + 1],
                                   ALU.pow).then_inc(rstd_ready, 1)

        @block.scalar
        def _(act):
            def transposed_hi(*blocks):
                for i in blocks:
                    b = i % NB
                    act.wait_ge(tp_done, i + 1)
                    act.activation(xt_hi[:, :, b * TB:(b + 1) * TB],
                                   r_ps[:, TP_BANK[i], 0:DK * TB].rearrange("p (k n) -> p k n", k=DK),
                                   ACT.Copy).then_inc(xt_hi_ready, 1)

            def far(*steps):
                for i in steps:
                    if i >= OH_STEPS:
                        act.wait_ge(oh_used, i - (OH_STEPS - 1))
                    for r in range(ACT_ROWS[i]):
                        n = sum(ACT_ROWS[:i]) + r
                        c = STEP - ACT_ROWS[i] + r
                        col = slice(STEP * i + c, STEP * i + c + 1)
                        if n >= 2:
                            act.wait_ge(oh_far_ready, n - 1)
                        act.activation(distance[:, n % 2, :], iota_src[:, 0:OW], ACT.Abs,
                                       bias=dst_lo_neg[:, col]).then_inc(distance_ready, 1)
                        act.wait_ge(distance_ready, n + 1)
                        act.activation(oh_dst[:, i % OH_STEPS * STEP + c, :], distance[:, n % 2, :], ACT.Relu,
                                       bias=dst_val[:, col], scale=dst_val_neg[:, col]).then_inc(oh_far_ready, 1)

            def upper_counts(gr):
                for jb in range(NB):
                    if jb < NB - 1:
                        act.wait_ge(cnt_done, (NB - 1) * gr + jb + 1)
                    else:
                        act.wait_ge(oh_used, sum(GROUPS[:gr + 1]))
                    if gr >= 1 and jb == 0:
                        act.wait_ge(counts_read, NB * gr)
                        act.wait_ge(up_added, NB * gr)
                    act.activation(count_up[:, jb, :], y_ps[0:TB, jb, 0:OW], ACT.Copy, scale=1.0 / FIELD,
                                   bias=-ROUND_DOWN).then_inc(count_up_ready, 1)

            def weight_hi(*pieces):
                for m in pieces:
                    act.activation(w_hi[0][:, m, :], w_raw[0][:, m, :], ACT.Copy).then_inc(w_hi_ready, 1)

            def h_hi_part(b):
                act.wait_ge(hg_ready, b + 1)
                act.activation(hg_hi[:, b, :], h[:, b % 2, :], ACT.Copy).then_inc(hg_hi_ready, 1)

            def exponentials(jb):
                act.activation(ex_lin[:, jb, :], s_bc[:], ACT.Exp, bias=s_src_b[:, jb:jb + 1]).then_inc(ex_ready, 1)
                if jb >= 2:
                    act.wait_ge(ex_max, jb - 1)
                act.activation(ex_sl[:, jb % 2, :], s_bc[:], ACT.Exp, bias=s_src_s[:, jb:jb + 1],
                               scale=SLOPE).then_inc(ex_ready, 1)

            act.wait_ge(iota_ready, 1)
            act.wait_ge(keys_ready, 1)
            far(0, 1, 2, 3)
            act.wait_ge(shift_ready, 1)
            for b in range(NB):
                act.activation(xn[:, b, :], acc[:, b, :], ACT.Identity, bias=shift[:, b:b + 1],
                               scale=rstd[:, b:b + 1]).then_inc(xn_ready, 1)
            far(4, 5)
            transposed_hi(0, 1, 2)
            act.wait_ge(wg_in, 16)
            for k in range(DK):
                act.activation(wg_hi[:, k, :], wg_raw[:, k, :], ACT.Copy).then_inc(wg_hi_ready, 1)
                if k == 1:
                    transposed_hi(3, 4)
            far(6, 7, 8)
            upper_counts(0)
            far(9)
            h_hi_part(0)
            far(10)
            h_hi_part(1)
            act.wait_ge(w_in[0], 32)
            weight_hi(0, 1)
            far(11)
            h_hi_part(2)
            weight_hi(2, 3)
            far(12)
            h_hi_part(3)
            weight_hi(4, 5)
            far(13)
            h_hi_part(4)
            weight_hi(6, 7)
            act.wait_ge(ffn_vec_in, 48)
            act.activation(rwt_hi[:], rwt[:], ACT.Copy).then_inc(rt_hi_ready, 1)
            far(14)
            act.wait_ge(sbc_done, 1)
            act.wait_ge(consts_ready, CONSTS)
            act.activation(s_bc[:, 0:4 * TB], r_ps[0:TB, 1, 0:4 * TB], ACT.Copy).then_inc(sbc_copied, 1)
            act.activation(s_bc[:, 4 * TB:N], r_ps[0:TB, 2, 0:TB], ACT.Copy).then_inc(sbc_copied, 1)
            far(15)
            upper_counts(1)
            far(16)
            act.wait_ge(sbc_copied, 2)
            act.wait_ge(scores_ready, 1)
            exponentials(0)
            far(17)
            exponentials(1)
            far(18)
            exponentials(2)
            far(19)
            exponentials(3)
            exponentials(4)
            upper_counts(2)
            for jb in range(NB):
                act.wait_ge(attn_ready, jb + 1)
                act.activation(attn_hi[:, jb, :], ex_lin[:, jb, :], ACT.Copy).then_inc(attn_hi_ready, 1)
            transposed_hi(*range(NB, 2 * NB))
            act.wait_ge(rb_ready, 1)
            for hf, (n0, nw) in enumerate(HALVES):
                act.wait_ge(router_done, hf + 1)
                w = min(nw, N - n0)
                act.activation(e_neg_t[:, n0:n0 + w], y_ps[0:7, hf, 0:w], ACT.Exp, bias=rb_neg[:],
                               scale=-1.0).then_inc(e_neg_ready, 1)

            def expert(e, last):
                act.wait_ge(b1_ready, e + 1)
                for c in range(CH):
                    for t in range(TC):
                        j = TC * c + t
                        for hf, (n0, nw) in enumerate(HALVES):
                            u = 2 * j + hf
                            act.wait_ge(h_done, e * UNITS + u + 1)
                            if j >= 2:
                                act.wait_ge(h_ready, e * UNITS + u - 3)
                            act.activation(g[:, j % 2, n0:n0 + nw], r_ps[:, u % 3, 0:nw], ACT.Gelu,
                                           bias=b1_now[:, j:j + 1]).then_inc(gelu_done, 1)
                        if last and c == CH - 1:
                            continue
                        for m in (2 * t, 2 * t + 1):
                            s = (c + 1) % 2
                            if m == 0:
                                act.wait_ge(w_in[s], e * (32 * CH // 2) + 32 * ((c + 1) // 2 + 1))
                            if c == CH - 1 and m == PIECES - 1:
                                act.wait_ge(gelu_done, e * UNITS + UNITS)
                            act.activation(w_hi[s][:, m, :], w_raw[s][:, m, :], ACT.Copy).then_inc(w_hi_ready, 1)
                if not last:
                    act.activation(b1_now[:], b1_sb[:, bass.ds(e * HT + HT, HT)], ACT.Copy).then_inc(b1_ready, 1)

            act.activation(b1_now[:], b1_sb[:, 0:HT], ACT.Copy).then_inc(b1_ready, 1)
            with act.Fori(0, E - 1) as e:
                expert(e, False)
            expert(E - 1, True)

        @block.vector
        def _(dve):
            seq = [0]

            def landed():
                seq[0] += 1
                return seq[0]

            def layernorm_stats(b):
                dve.bn_stats(stats[:, b, :], acc[:, b, :]).then_inc(dve_seq, 1)
                dve.wait_ge(dve_seq, landed())
                dve.bn_aggr(moments[:, b, :], stats[:, b, :]).then_inc(dve_seq, 1)
                dve.wait_ge(dve_seq, landed())

            def layernorm_apply(b):
                dve.tensor_scalar(xn[:, b, :], acc[:, b, :], moments[:, b, 0:1], rstd[:, b:b + 1],
                                  ALU.subtract, ALU.mult).then_inc(xn_ready, 1)

            def transposed_lo(i):
                b = i % NB
                dve.wait_ge(xt_hi_ready, i + 1)
                dve.tensor_tensor(xt_lo[:, :, b * TB:(b + 1) * TB],
                                  r_ps[:, TP_BANK[i], 0:DK * TB].rearrange("p (k n) -> p k n", k=DK),
                                  xt_hi[:, :, b * TB:(b + 1) * TB].bitcast(F32), ALU.subtract).then_inc(xt_ready, 1)

            def one_hot_step(i):
                if i >= OH_STEPS:
                    dve.wait_ge(oh_used, i - (OH_STEPS - 1))
                for c in range(STEP):
                    s = i % OH_STEPS * STEP + c
                    col = slice(i * STEP + c, i * STEP + c + 1)
                    one_hot = dve.tensor_scalar(oh_src[:, s, :], iota_src[:], edge_f[:, 0, col], None, ALU.is_equal)
                    if c >= STEP - ACT_ROWS[i]:
                        one_hot.then_inc(oh_ready, 1)
                        continue
                    dve.tensor_scalar(oh_dst[:, s, :], iota_src[:, 0:OW], dst_lo[:, col], dst_val[:, col],
                                      ALU.is_equal, ALU.mult).then_inc(oh_ready, 1)

            def lower_count(gr, jb):
                dve.wait_ge(count_up_ready, NB * gr + jb + 1)
                low = count[:, jb, 0, :] if gr == 0 else count_dn[:, jb, :]
                dve.scalar_tensor_tensor(low, count_up[:, jb, :], -FIELD, y_ps[0:TB, jb, 0:OW],
                                         ALU.mult, ALU.add).then_inc(counts_read, 1)

            def scores(b):
                dve.wait_ge(hg_done, b + 1)
                if b >= 2:
                    dve.wait_ge(hg_lo_ready, b - 1)
                dve.tensor_tensor(h[:, b % 2, :], r_ps[0:TB, (b + 2) % 3, :], bw_bc, ALU.add).then_inc(hg_ready, 1)
                dve.wait_ge(hg_ready, b + 1)
                for s, half in ((s_dst, 0), (s_src, 1)):
                    dve.tensor_tensor_reduce(out=scratch, in0=h[:, b % 2, :], in1=a_bc[:, half, :], scale=1.0,
                                             scalar=0.0, op0=ALU.mult, op1=ALU.add,
                                             accum_out=s[:, b:b + 1]).then_inc(dve_seq, 1)
                    dve.wait_ge(dve_seq, landed())

            def exp_max(jb):
                dve.wait_ge(ex_ready, 2 * jb + 2)
                dve.tensor_tensor(ex_lin[:, jb, :], ex_lin[:, jb, :], ex_sl[:, jb % 2, :], ALU.max).then_inc(ex_max, 1)

            dve.wait_ge(edges_in, 32)
            dve.tensor_copy(edge_f[:], edge_i[:]).then_inc(dve_seq, 1)
            dve.wait_ge(dve_seq, landed())
            dve.tensor_scalar(upper[:], edge_f[:, 1, :], float(LO_N), None, ALU.is_ge).then_inc(dve_seq, 1)
            dve.wait_ge(dve_seq, landed())
            dve.scalar_tensor_tensor(dst_lo[:], upper[:], -float(LO_N), edge_f[:, 1, :], ALU.mult,
                                     ALU.add).then_inc(dve_seq, 1)
            landed()
            dve.tensor_scalar(dst_val[:], upper[:], FIELD - 1.0, 1.0, ALU.mult, ALU.add).then_inc(dve_seq, 1)
            landed()
            dve.wait_ge(dve_seq, seq[0])
            dve.tensor_scalar(dst_lo_neg[:], dst_lo[:], -1.0, None, ALU.mult)
            dve.tensor_scalar(dst_val_neg[:], dst_val[:], -1.0, None, ALU.mult).then_inc(keys_ready, 1)
            dve.wait_ge(iota_ready, 1)
            one_hot_step(0)
            one_hot_step(1)

            dve.wait_ge(x_in, 16)
            for b in range(NB):
                dve.bn_stats(stats[:, b, :], acc[:, b, :]).then_inc(dve_seq, 1)
                landed()
            dve.wait_ge(dve_seq, seq[0])
            for b in range(NB):
                dve.bn_aggr(moments[:, b, :], stats[:, b, :]).then_inc(dve_seq, 1)
                landed()
            dve.wait_ge(dve_seq, seq[0])
            dve.tensor_scalar(var_eps[:], moments[:, :, 1], EPS, None, ALU.add).then_inc(ve_ready, 1)
            one_hot_step(2)
            dve.wait_ge(rstd_ready, 1)
            dve.scalar_tensor_tensor(shift[:], moments[:, :, 0], -1.0, rstd[:], ALU.mult, ALU.mult).then_inc(shift_ready, 1)
            for i in range(3, 6):
                one_hot_step(i)
            for b in range(3):
                transposed_lo(b)
            one_hot_step(6)
            transposed_lo(3)
            transposed_lo(4)
            one_hot_step(7)
            one_hot_step(8)
            for jb in range(NB):
                lower_count(0, jb)
            dve.wait_ge(vec_in, 64)
            for b in range(NB):
                one_hot_step(9 + b)
                scores(b)
            for b in range(NB):
                dve.tensor_scalar(diag[:, b, :], ident[0:TB, 0:TB], s_dst[:, b:b + 1], None,
                                  ALU.mult).then_inc(diag_ready, 1)
            dve.tensor_scalar(s_src_b[:], s_src[:], ba_bc[:, 0:1], None, ALU.add).then_inc(dve_seq, 1)
            dve.wait_ge(dve_seq, landed())
            dve.tensor_scalar(s_src_s[:], s_src_b[:], SLOPE, None, ALU.mult).then_inc(scores_ready, 1)
            one_hot_step(14)
            one_hot_step(15)
            for jb in range(NB):
                lower_count(1, jb)
            one_hot_step(16)
            one_hot_step(17)
            exp_max(0)
            one_hot_step(18)
            exp_max(1)
            one_hot_step(19)
            for jb in range(2, NB):
                exp_max(jb)
            def weights(jb):
                dve.wait_ge(up_added, 2 * NB + jb + 1)
                dve.wait_ge(dn_added, NB + jb + 1)
                w = ex_lin[:, jb, :].rearrange("p (f n) -> p f n", f=2)
                dve.scalar_tensor_tensor(w, w, FLT_MAX, count[:, jb, :, 0:LO_N], ALU.min, ALU.mult).then_inc(attn_ready, 1)

            def weights_lo(jb):
                dve.wait_ge(attn_hi_ready, jb + 1)
                dve.tensor_tensor(attn_lo[:, jb, :], ex_lin[:, jb, :], attn_hi[:, jb, :].bitcast(F32),
                                  ALU.subtract).then_inc(attn_lo_ready, 1)

            dve.wait_ge(dn_added, NB)
            lower_count(2, 0)
            for jb in range(NB):
                if jb + 1 < NB:
                    lower_count(2, jb + 1)
                if jb == 1:
                    dve.wait_ge(oh_used, sum(GROUPS))
                if jb >= 1:
                    weights_lo(jb - 1)
                weights(jb)
            weights_lo(NB - 1)
            dve.wait_ge(ffn_vec_in, 48)
            dve.tensor_scalar(rb_neg[:], rb_col[:], -1.0, None, ALU.mult).then_inc(rb_ready, 1)
            def second_layernorm(b):
                dve.wait_ge(agg_done, b + 1)
                dve.scalar_tensor_tensor(acc[:, b, :], y_ps[0:TB, b, :], rden[:, b:b + 1], acc[:, b, :],
                                         ALU.mult, ALU.add).then_inc(y_added, 1)
                dve.wait_ge(y_added, b + 1)
                layernorm_stats(b)
                dve.tensor_scalar(var_eps[:, b:b + 1], moments[:, b, 1:2], EPS, None, ALU.add).then_inc(ve_ready, 1)

            def denominators(first, last):
                blocks = slice(first, last)
                dve.wait_ge(den_read, last)
                dve.scalar_tensor_tensor(den_safe[:, blocks], den[:, blocks], 0.0, den[:, blocks],
                                         ALU.is_equal, ALU.add).then_inc(dve_seq, 1)
                dve.wait_ge(dve_seq, landed())
                dve.reciprocal(rden[:, blocks], den_safe[:, blocks]).then_inc(dve_seq, 1)
                dve.wait_ge(dve_seq, landed())

            for b in range(3):
                dve.wait_ge(den_done, b + 1)
                dve.tensor_copy(den[:, b:b + 1], r_ps[0:TB, b, 0:1]).then_inc(den_read, 1)
            denominators(0, 3)
            def second_apply(b):
                dve.wait_ge(rstd_ready, 2 + b)
                layernorm_apply(b)

            second_layernorm(0)
            second_layernorm(1)
            second_apply(0)
            second_layernorm(2)
            second_apply(1)
            second_apply(2)
            dve.wait_ge(den_done, NB)
            for ib in (3, 4):
                dve.tensor_copy(den[:, ib:ib + 1], r_ps[0:TB, 0, 2 * ib:2 * ib + 1]).then_inc(den_read, 1)
            denominators(3, NB)
            second_layernorm(3)
            transposed_lo(NB)
            second_apply(3)
            transposed_lo(NB + 1)
            transposed_lo(NB + 2)
            second_layernorm(4)
            transposed_lo(NB + 3)
            second_apply(4)
            transposed_lo(NB + 4)
            dve.wait_ge(tree_done, 1)
            dve.tensor_scalar(one_plus[:], y_ps[0:TB, 2, 0:8 * NB].rearrange("p (b n) -> p b n", b=NB)[:, :, 0:7], 1.0,
                              None, ALU.add).then_inc(tree_read, 1)
            dve.wait_ge(tree_read, 1)
            dve.reciprocal(prob[:, :, :, 1], one_plus[:]).then_inc(dve_seq, 1)
            dve.wait_ge(dve_seq, landed())
            dve.tensor_scalar(prob[:, :, :, 0], prob[:, :, :, 1], -1.0, 1.0, ALU.mult, ALU.add).then_inc(dve_seq, 1)
            dve.wait_ge(dve_seq, landed())
            for m in range(4):
                dve.tensor_tensor(pair[:, :, m], prob[:, :, 0, m // 2], prob[:, :, 1 + m // 2, m % 2],
                                  ALU.mult).then_inc(dve_seq, 1)
                landed()
            dve.wait_ge(dve_seq, seq[0])
            for n in range(E):
                dve.tensor_tensor(leaf[:, :, n], pair[:, :, n // 2], prob[:, :, 3 + n // 2, n % 2],
                                  ALU.mult).then_inc(dve_seq, 1)
                landed()
            dve.wait_ge(dve_seq, seq[0])

            def expert(e, last):
                for c in range(CH):
                    for t in range(TC):
                        j = TC * c + t
                        for hf, (n0, nw) in enumerate(HALVES):
                            u = 2 * j + hf
                            cols = slice(n0, n0 + nw)
                            dve.wait_ge(gelu_done, e * UNITS + u + 1)
                            if hf == 0 and j >= 2:
                                dve.wait_ge(l2_done, e * (HT - 1) + j - 1)
                            dve.tensor_copy(h_hi[:, j % 2, cols], g[:, j % 2, cols]).then_inc(h_hi_ready, 1)
                            dve.wait_ge(h_hi_ready, e * UNITS + u + 1)
                            dve.tensor_tensor(h_lo[:, j % 2, cols], g[:, j % 2, cols],
                                              h_hi[:, j % 2, cols].bitcast(F32), ALU.subtract).then_inc(h_ready, 1)
                        if 2 <= j < 2 + NB:
                            b = j - 2
                            if b == 0:
                                dve.wait_ge(b2_in, 16)
                                dve.wait_ge(y_added, e * NB + NB)
                            dve.scalar_tensor_tensor(acc[:, b, :], b2_bc[:, bass.ds(e, 1), :].rearrange("p e d -> p (e d)"),
                                                     leaf[:, b, bass.ds(e, 1)], acc[:, b, :],
                                                     ALU.mult, ALU.add).then_inc(b2_added, 1)
                        if last and c == CH - 1:
                            continue
                        for m in (2 * t, 2 * t + 1):
                            s = (c + 1) % 2
                            dve.wait_ge(w_hi_ready, e * (CH * PIECES) + PIECES * (c + 1) + m + 1)
                            dve.tensor_tensor(w_lo[s][:, m, :], w_raw[s][:, m, :], w_hi[s][:, m, :].bitcast(F32),
                                              ALU.subtract).then_inc(w_ready, 1)
                dve.wait_ge(b2_added, e * NB + NB)
                for b in range(NB):
                    dve.wait_ge(y_done, e * NB + b + 1)
                    dve.scalar_tensor_tensor(acc[:, b, :], y_ps[0:TB, b, :], leaf[:, b, bass.ds(e, 1)], acc[:, b, :],
                                             ALU.mult, ALU.add).then_inc(y_added, 1)

            with dve.Fori(0, E - 1) as e:
                expert(e, False)
            expert(E - 1, True)

        @block.tensor
        def _(pe):
            def product(out_ap, lhs, rhs, start, stop):
                pe.matmul(out_ap, lhs[0], rhs[0], start=start, stop=False)
                pe.matmul(out_ap, lhs[0], rhs[1], start=False, stop=False)
                return pe.matmul(out_ap, lhs[1], rhs[0], start=False, stop=stop)

            def transpose_block(i):
                b = i % NB
                pe.wait_ge(xn_ready, i + 1)
                for k in range(DK):
                    m = pe.transpose(r_ps[:, TP_BANK[i], k * TB:(k + 1) * TB], xn[:, b, k * P:(k + 1) * P],
                                     ident[0:TB, 0:TB])
                m.then_inc(tp_done, 1)

            def count_step(i, gr, first=False, last=False):
                def count(jb, c):
                    s = i % OH_STEPS * STEP + c
                    return pe.matmul(y_ps[0:TB, jb, 0:OW], oh_src[:, s, jb * TB:(jb + 1) * TB], oh_dst[:, s, :],
                                     start=first and c == 0, stop=last and c == STEP - 1)

                if i == 0:
                    for c in range(STEP):
                        pe.wait_ge(oh_ready, c + 1)
                        if c == STEP - ACT_ROWS[0]:
                            pe.wait_ge(oh_far_ready, ACT_ROWS[0])
                        for jb in range(NB):
                            m = count(jb, c)
                    m.then_inc(oh_used, 1)
                    return
                pe.wait_ge(oh_ready, (i + 1) * STEP)
                pe.wait_ge(oh_far_ready, sum(ACT_ROWS[:i + 1]))
                for jb in range(NB):
                    if gr >= 1 and first:
                        pe.wait_ge(counts_read, NB * (gr - 1) + jb + 1)
                    for c in range(STEP):
                        m = count(jb, c)
                        if last and c == STEP - 1 and jb < NB - 1:
                            m.then_inc(cnt_done, 1)
                m.then_inc(oh_used, 1)

            def hidden_graph(b):
                if b < 3:
                    pe.wait_ge(xt_ready, b + 3)
                else:
                    pe.wait_ge(hg_ready, b - 2)
                for k in range(DK):
                    cols = slice(b * TB, (b + 1) * TB)
                    m = product(r_ps[0:TB, (b + 2) % 3, :], (xt_hi[:, k, cols], xt_lo[:, k, cols]),
                                (wg_hi[:, k, :], wg_lo[:, k, :]), k == 0, k == DK - 1)
                m.then_inc(hg_done, 1)

            pe.wait_ge(consts_ready, CONSTS)
            count_step(0, 0, first=True)
            for i in range(1, 4):
                count_step(i, 0)
            for b in range(3):
                transpose_block(b)
            count_step(4, 0)
            for b in (3, 4):
                pe.wait_ge(xt_ready, b - 2)
                transpose_block(b)
            count_step(5, 0)
            count_step(6, 0, last=True)
            pe.wait_ge(wg_ready, DK)
            for b in range(NB):
                hidden_graph(b)
                count_step(7 + b, 1, first=b == 0)
            count_step(12, 1)
            pe.wait_ge(hg_ready, NB - 1)
            for b in range(NB):
                pe.wait_ge(diag_ready, b + 1)
                m = pe.matmul(r_ps[0:TB, 1 + b // 4, (b % 4) * TB:(b % 4 + 1) * TB], ones_f[:], diag[:, b, :],
                              start=True, stop=True)
            m.then_inc(sbc_done, 1)
            count_step(13, 1, last=True)
            count_step(14, 2, first=True)
            for i in range(15, 19):
                count_step(i, 2)
            count_step(19, 2, last=True)

            def attend(ib, jb, parts):
                cols = slice(ib * TB, (ib + 1) * TB)
                if 0 in parts:
                    pe.matmul(y_ps[0:TB, ib, :], attn_hi[:, jb, cols], hg_hi[:, jb, :], start=jb == 0, stop=False)
                    m = pe.matmul(y_ps[0:TB, ib, :], attn_hi[:, jb, cols], hg_lo[:, jb, :], start=False, stop=False)
                if 1 in parts:
                    m = pe.matmul(y_ps[0:TB, ib, :], attn_lo[:, jb, cols], hg_hi[:, jb, :], start=False,
                                  stop=jb == NB - 1)
                return m

            def denominator(ib, jb, out_ap):
                return pe.matmul(out_ap, ex_lin[:, jb, ib * TB:(ib + 1) * TB], ones_f[:, 0:2],
                                 start=jb == 0, stop=jb == NB - 1)

            pe.wait_ge(hg_lo_ready, NB)
            pe.wait_ge(sbc_copied, 2)
            for jb in range(NB):
                pe.wait_ge(attn_ready, jb + 1)
                for ib in range(3):
                    m = denominator(ib, jb, r_ps[0:TB, ib, 0:2])
                    if jb == NB - 1:
                        m.then_inc(den_done, 1)
                pe.wait_ge(attn_hi_ready, jb + 1)
                for ib in range(3):
                    pe.wait_ge(counts_read, 2 * NB + ib + 1)
                    attend(ib, jb, (0,))
                pe.wait_ge(attn_lo_ready, jb + 1)
                for ib in range(3):
                    m = attend(ib, jb, (1,))
                    if jb == NB - 1:
                        m.then_inc(agg_done, 1)
            pe.wait_ge(den_read, 3)
            for ib in (3, 4):
                for jb in range(NB):
                    m = denominator(ib, jb, r_ps[0:TB, 0, 2 * ib:2 * ib + 2])
                m.then_inc(den_done, 1)
            pe.wait_ge(counts_read, 3 * NB)
            for jb in range(NB):
                m = attend(3, jb, (0, 1))
            m.then_inc(agg_done, 1)
            transpose_block(NB)
            transpose_block(NB + 1)
            for jb in range(NB):
                m = attend(4, jb, (0, 1))
            m.then_inc(agg_done, 1)

            def router(hf):
                n0, nw = HALVES[hf]
                pe.wait_ge(y_added, hf + 1)
                for k in range(DK):
                    cols = slice(n0, n0 + nw)
                    m = product(y_ps[:, hf, 0:nw], (rwt_hi[:, k, :], rwt_lo[:, k, :]),
                                (xt_hi[:, k, cols], xt_lo[:, k, cols]), k == 0, k == DK - 1)
                m.then_inc(router_done, 1)

            pe.wait_ge(den_read, NB)
            transpose_block(NB + 2)
            pe.wait_ge(xt_ready, NB + 1)
            transpose_block(NB + 3)
            pe.wait_ge(rt_ready, 1)
            pe.wait_ge(xt_ready, NB + 3)
            router(0)

            def tree():
                pe.wait_ge(y_added, 3)
                pe.wait_ge(e_neg_ready, 2)
                for b in range(NB):
                    m = pe.transpose(y_ps[0:TB, 2, 8 * b:8 * b + 7], e_neg_t[:, b * TB:(b + 1) * TB], ident[0:7, 0:7])
                m.then_inc(tree_done, 1)

            def hidden(e, j, halves=(0, 1)):
                s, t = (j // TC) % 2, j % TC
                if t == 0:
                    pe.wait_ge(w_ready, e * (CH * PIECES) + PIECES * (j // TC) + DK)
                for hf in halves:
                    n0, nw = HALVES[hf]
                    u = 2 * j + hf
                    if u >= 3:
                        pe.wait_ge(gelu_done, e * UNITS + u - 2)
                    for k in range(DK):
                        cols = slice(n0, n0 + nw)
                        wc = slice(t * P, (t + 1) * P)
                        m = product(r_ps[:, u % 3, 0:nw], (w_hi[s][:, k, wc], w_lo[s][:, k, wc]),
                                    (xt_hi[:, k, cols], xt_lo[:, k, cols]), k == 0, k == DK - 1)
                    m.then_inc(h_done, 1)

            def output(e, j):
                s, t = (j // TC) % 2, j % TC
                pe.wait_ge(w_ready, e * (CH * PIECES) + PIECES * (j // TC) + DK + t + 1)
                pe.wait_ge(h_ready, e * UNITS + 2 * j + 2)
                if j == 0:
                    pe.wait_ge(y_added, e * NB + NB)
                    pe.wait_ge(tree_read, 1)
                for b in range(NB):
                    cols = slice(b * TB, (b + 1) * TB)
                    m = product(y_ps[0:TB, b, :], (h_hi[:, j % 2, cols], h_lo[:, j % 2, cols]),
                                (w_hi[s][:, DK + t, :], w_lo[s][:, DK + t, :]), j == 0, j == HT - 1)
                    if j == HT - 1:
                        m.then_inc(y_done, 1)
                if j < HT - 1:
                    m.then_inc(l2_done, 1)

            def expert_rest(e):
                for j in range(1, HT):
                    if j >= 2:
                        hidden(e, j)
                    output(e, j - 1)
                output(e, HT - 1)

            hidden(0, 0, (0,))
            pe.wait_ge(xt_ready, NB + 2)
            transpose_block(NB + 4)
            pe.wait_ge(xt_ready, NB + 5)
            router(1)
            hidden(0, 0, (1,))
            tree()
            hidden(0, 1)
            expert_rest(0)
            with pe.Fori(1, E) as e:
                hidden(e, 0)
                hidden(e, 1)
                expert_rest(e)


TP_BANK = (0, 1, 2, 0, 1, 1, 2, 0, 1, 2)


def kernel(x, src, dst, L0_gnn_W, L0_gnn_b_w, L0_gnn_a, L0_gnn_b_a, L0_ffn_rw, L0_ffn_rb, L0_ffn_w1, L0_ffn_b1,
           L0_ffn_w2, L0_ffn_b2):
    import numpy as np
    import concourse.bacc as bacc
    from concourse.bass_utils import run_bass_kernel_spmd

    rw = np.asarray(L0_ffn_rw)
    rw_t = rw.reshape(rw.shape[0], DK, P).transpose(2, 1, 0).reshape(P, -1)
    b1_t = np.asarray(L0_ffn_b1).reshape(E * HT, P).T
    ins = {
        "x": x, "src": src, "dst": dst, "w_gnn": L0_gnn_W, "b_w": L0_gnn_b_w, "a_vec": L0_gnn_a,
        "b_a": np.asarray(L0_gnn_b_a).reshape(1), "rw_t": rw_t, "rb": L0_ffn_rb, "w1": L0_ffn_w1, "b1_t": b1_t,
        "w2": L0_ffn_w2, "b2": L0_ffn_b2,
    }
    nc = bacc.Bacc("TRN2", target_bir_lowering=False, num_devices=1)
    arrays, args = {}, {}
    for name, value in ins.items():
        value = np.ascontiguousarray(value)
        arrays[f"in_{name}"] = value
        args[name] = nc.dram_tensor(f"in_{name}", value.shape, mybir.dt.from_np(value.dtype), kind="ExternalInput").ap()
    args["out"] = nc.dram_tensor("out_x", (N, D), F32, kind="ExternalOutput").ap()
    gnn_ffn_kernel(nc, **args)
    result = run_bass_kernel_spmd(nc, [arrays], core_ids=[0])
    return result.results[0]["out_x"]
```

```python
from contextlib import ExitStack

import concourse.bass as bass
from concourse import mybir

ALU = mybir.AluOpType
ACT = mybir.ActivationFunctionType
F32 = mybir.dt.float32
F32R = mybir.dt.float32r
F16 = mybir.dt.float16
I32 = mybir.dt.int32

P = 128
N = 625
TB = 125
NB = N // TB
D = 512
DK = D // P
E = 8
HID = 2048
HT = HID // P
CW = 512
CH = HID // CW
TC = CW // P
NP = N + 1
HALVES = ((0, 314), (314, 312))
UNITS = 2 * HT
PIECES = DK + TC
EPS = 1e-5
SLOPE = 0.2
FLT_MAX = 3.4028234663852886e38

EDGES = 10000
EC = EDGES // TB
LO_N = 313
OW = 314
SW = 626
FIELD = 4096.0
FIELD_BITS = 12
STEP = 4
OH_STEPS = 3
GROUPS = (7, 7, 6)
ACT_ROWS = (1, 1, 2, 2, 2, 1, 1, 0, 0) + (1,) * 10 + (0,)
WARM_UP = 9
CONSTS = 8
assert sum(GROUPS) * STEP == EC and max(GROUPS) * STEP * TB < FIELD



def gnn_ffn_kernel(nc, x, src, dst, w_gnn, b_w, a_vec, b_a, rw_t, rb, w1, b1_t, w2, b2, out):
    with ExitStack() as ctx:
        def sb(scope, name, shape, dt=F32):
            return scope.enter_context(nc.sbuf_tensor(name, shape, dt))

        def sem(name):
            return ctx.enter_context(nc.semaphore(name))

        y_ps = ctx.enter_context(nc.psum_tensor("y_ps", [P, NB, 512], F32))
        r_ps = ctx.enter_context(nc.psum_tensor("r_ps", [P, 3, 512], F32))

        acc = sb(ctx, "acc", [TB, NB, D])
        xn = sb(ctx, "xn", [TB, NB, D])
        xt_hi = sb(ctx, "xt_hi", [P, DK, NP], F32R)
        xt_lo = sb(ctx, "xt_lo", [P, DK, NP], F32R)
        ident = sb(ctx, "ident", [P, P])
        stats = sb(ctx, "stats", [TB, NB, 6])
        moments = sb(ctx, "moments", [TB, NB, 2])
        var_eps = sb(ctx, "var_eps", [TB, NB])
        minus_half = sb(ctx, "minus_half", [TB, NB])
        rstd = sb(ctx, "rstd", [TB, NB])
        leaf = sb(ctx, "leaf", [TB, NB, E])
        rb_col = sb(ctx, "rb_col", [7, 1])
        rb_neg = sb(ctx, "rb_neg", [7, 1])
        e_neg_t = sb(ctx, "e_neg_t", [7, NP])
        one_plus = sb(ctx, "one_plus", [TB, NB, 7])
        prob = sb(ctx, "prob", [TB, NB, 7, 2])
        pair = sb(ctx, "pair", [TB, NB, 4])
        b1_sb = sb(ctx, "b1_sb", [P, E * HT])
        b1_now = sb(ctx, "b1_now", [P, HT])
        w_raw = [sb(ctx, "w_raw0", [P, PIECES, CW])]
        w_hi = [sb(ctx, "w_hi0", [P, PIECES, CW], F32R)]
        w_lo = [sb(ctx, "w_lo0", [P, PIECES, CW], F32R)]

        with ExitStack() as gnn:
            wg_raw = w_raw[0][:, 0:DK, :]
            count = sb(gnn, "count", [TB, NB, 2, OW], I32)
            hg_hi = sb(gnn, "hg_hi", [TB, NB, D], F32R)
            hg_lo = sb(gnn, "hg_lo", [TB, NB, D], F32R)
            h = xn[:, 0:2, :]
            a_bc = xn[:, 2:4, :]
            bw_bc = xn[:, 4, :]
            rwt = sb(gnn, "rwt", [P, DK, P])
            rwt_hi = sb(gnn, "rwt_hi", [P, DK, P], F32R)
            rwt_lo = sb(gnn, "rwt_lo", [P, DK, P], F32R)
            ba_bc = sb(gnn, "ba_bc", [TB, 1])
            s_dst = sb(gnn, "s_dst", [TB, NB])
            s_src = sb(gnn, "s_src", [TB, NB])
            s_src_b = sb(gnn, "s_src_b", [TB, NB])
            s_src_s = sb(gnn, "s_src_s", [TB, NB])
            s_bc = sb(gnn, "s_bc", [TB, NP])
            ex_lin = sb(gnn, "ex_lin", [TB, NB, NP])
            ex_sl = sb(gnn, "ex_sl", [TB, 2, NP])
            scratch = ex_sl[:, 0, 0:D]
            diag = ex_sl[:, 1, 0:N].rearrange("p (b n) -> p b n", b=NB)
            ones_f = sb(gnn, "ones_f", [TB, TB])
            iota_src = sb(gnn, "iota_src", [TB, SW], F16)
            edge_i = sb(gnn, "edge_i", [TB, 2, EC], I32)
            edge_f = sb(gnn, "edge_f", [TB, 2, EC])
            upper = sb(gnn, "upper", [TB, EC])
            dst_lo = sb(gnn, "dst_lo", [TB, EC])
            dst_val = sb(gnn, "dst_val", [TB, EC])
            dst_lo_neg = sb(gnn, "dst_lo_neg", [TB, EC])
            dst_val_neg = sb(gnn, "dst_val_neg", [TB, EC])
            distance = sb(gnn, "distance", [TB, 2, OW], F16)
            neg_mean = sb(gnn, "neg_mean", [TB, NB])
            shift = sb(gnn, "shift", [TB, NB])
            packed = sb(gnn, "packed", [TB, NB, OW], I32)
            count_dn = sb(gnn, "count_dn", [TB, NB, OW], I32)
            den = sb(gnn, "den", [TB, NB])
            den_safe = sb(gnn, "den_safe", [TB, NB])
            rden = sb(gnn, "rden", [TB, NB])
            with ExitStack() as early:
                wg_hi = sb(early, "wg_hi", [P, DK, D], F32R)
                wg_lo = sb(early, "wg_lo", [P, DK, D], F32R)
                oh_src = sb(early, "oh_src", [TB, OH_STEPS * STEP, SW], F16)
                oh_dst = sb(early, "oh_dst", [TB, OH_STEPS * STEP, OW], F16)
            with ExitStack() as late:
                attn_hi = sb(late, "attn_hi", [TB, NB, NP], F32R)
                attn_lo = sb(late, "attn_lo", [TB, NB, NP], F32R)
        w_raw.append(sb(ctx, "w_raw1", [P, PIECES, CW]))
        w_hi.append(sb(ctx, "w_hi1", [P, PIECES, CW], F32R))
        w_lo.append(sb(ctx, "w_lo1", [P, PIECES, CW], F32R))
        b2_bc = sb(ctx, "b2_bc", [TB, E, D])
        g = sb(ctx, "g", [P, 2, NP])
        h_hi = sb(ctx, "h_hi", [P, 2, NP], F32R)
        h_lo = sb(ctx, "h_lo", [P, 2, NP], F32R)

        x_in = sem("x_in")
        edges_in = sem("edges_in")
        wg_in = sem("wg_in")
        vec_in = sem("vec_in")
        ffn_vec_in = sem("ffn_vec_in")
        b2_in = sem("b2_in")
        w_in = [sem("w_in0"), sem("w_in1")]
        out_written = sem("out_written")
        pool_seq = sem("pool_seq")
        consts_ready = sem("consts_ready")
        iota_ready = sem("iota_ready")
        dve_seq = sem("dve_seq")
        ve_ready = sem("ve_ready")
        rstd_ready = sem("rstd_ready")
        xn_ready = sem("xn_ready")
        tp_done = sem("tp_done")
        xt_hi_ready = sem("xt_hi_ready")
        xt_ready = sem("xt_ready")
        wg_hi_ready = sem("wg_hi_ready")
        wg_ready = sem("wg_ready")
        hg_done = sem("hg_done")
        oh_ready = sem("oh_ready")
        oh_far_ready = sem("oh_far_ready")
        distance_ready = sem("distance_ready")
        oh_used = sem("oh_used")
        up_ready = sem("up_ready")
        dn_ready = sem("dn_ready")
        up_added = sem("up_added")
        dn_added = sem("dn_added")
        first_dn_added = sem("first_dn_added")
        keys_ready = sem("keys_ready")
        packed_ready = sem("packed_ready")
        shift_ready = sem("shift_ready")
        hg_ready = sem("hg_ready")
        hg_hi_ready = sem("hg_hi_ready")
        hg_lo_ready = sem("hg_lo_ready")
        rb_ready = sem("rb_ready")
        tree_done = sem("tree_done")
        tree_read = sem("tree_read")
        cnt_done = sem("cnt_done")
        scores_ready = sem("scores_ready")
        diag_ready = sem("diag_ready")
        sbc_done = sem("sbc_done")
        sbc_copied = sem("sbc_copied")
        ex_max = sem("ex_max")
        ex_ready = sem("ex_ready")
        attn_ready = sem("attn_ready")
        attn_hi_ready = sem("attn_hi_ready")
        attn_lo_ready = sem("attn_lo_ready")
        agg_done = sem("agg_done")
        den_done = sem("den_done")
        den_read = sem("den_read")
        rt_hi_ready = sem("rt_hi_ready")
        rt_ready = sem("rt_ready")
        router_done = sem("router_done")
        e_neg_ready = sem("e_neg_ready")
        w_hi_ready = sem("w_hi_ready")
        w_ready = sem("w_ready")
        b1_ready = sem("b1_ready")
        h_done = sem("h_done")
        gelu_done = sem("gelu_done")
        h_hi_ready = sem("h_hi_ready")
        h_ready = sem("h_ready")
        l2_done = sem("l2_done")
        y_done = sem("y_done")
        y_added = sem("y_added")
        b2_added = sem("b2_added")

        w1_v = w1.rearrange("e (k p) n -> e p k n", p=P)
        w2_v = w2.rearrange("e (t p) n -> e p t n", p=P)

        block = ctx.enter_context(nc.Block())

        @block.sync
        def _(sp):
            sp.dma_start(edge_i[:, 0, :], src.rearrange("(p c) -> p c", c=EC)).then_inc(edges_in, 16)
            sp.dma_start(edge_i[:, 1, :], dst.rearrange("(p c) -> p c", c=EC)).then_inc(edges_in, 16)
            sp.dma_start(acc[:], x.rearrange("(b p) d -> p b d", p=TB)).then_inc(x_in, 16)
            sp.dma_start(wg_raw, w_gnn.rearrange("(k p) n -> p k n", p=P)).then_inc(wg_in, 16)

            def load_chunk(e, c):
                slot = c % 2
                sp.dma_start(w_raw[slot][:, 0:DK, :], w1_v[bass.ds(e, 1), :, :, c * CW:(c + 1) * CW]
                             .rearrange("e p k n -> p (e k) n")).then_inc(w_in[slot], 16)
                sp.dma_start(w_raw[slot][:, DK:PIECES, :], w2_v[bass.ds(e, 1), :, c * TC:(c + 1) * TC, :]
                             .rearrange("e p t n -> p (e t) n")).then_inc(w_in[slot], 16)

            sp.wait_ge(tp_done, NB)
            sp.dma_start(bw_bc[:], b_w.partition_broadcast(TB)).then_inc(vec_in, 16)
            sp.dma_start(a_bc[:, 0, :], a_vec[0:D].partition_broadcast(TB)).then_inc(vec_in, 16)
            sp.dma_start(a_bc[:, 1, :], a_vec[D:2 * D].partition_broadcast(TB)).then_inc(vec_in, 16)
            sp.dma_start(ba_bc[:], b_a.partition_broadcast(TB)).then_inc(vec_in, 16)
            sp.wait_ge(wg_ready, DK)
            load_chunk(0, 0)
            sp.wait_ge(consts_ready, CONSTS)
            sp.dma_start(rwt[:, :, 0:7], rw_t.rearrange("p (k n) -> p k n", k=DK)).then_inc(ffn_vec_in, 16)
            sp.dma_start(rb_col[:], rb.rearrange("(p n) -> p n", n=1)).then_inc(ffn_vec_in, 16)
            sp.dma_start(b1_sb[:], b1_t).then_inc(ffn_vec_in, 16)
            sp.wait_ge(agg_done, NB)
            sp.wait_ge(den_done, NB)
            sp.wait_ge(router_done, 2)
            load_chunk(0, 1)
            sp.dma_start(b2_bc[:].rearrange("p e d -> p (e d)"),
                         b2.rearrange("e d -> (e d)").partition_broadcast(TB)).then_inc(b2_in, 16)
            for c in (2, 3):
                sp.wait_ge(w_ready, PIECES * (c - 1))
                load_chunk(0, c)
            with sp.Fori(1, E) as e:
                for c in range(CH):
                    sp.wait_ge(w_ready, e * (CH * PIECES) + PIECES * (c - 1))
                    load_chunk(e, c)
            for b in range(NB):
                sp.wait_ge(y_added, NB * E + b + 1)
                sp.dma_start(out[b * TB:(b + 1) * TB, :], acc[:, b, :]).then_inc(out_written, 16)
            sp.wait_ge(out_written, 16 * NB)

        @block.gpsimd
        def _(pool):
            pool.iota(iota_src[:], [[1, SW]], base=0, channel_multiplier=0,
                      allow_small_or_imprecise_dtypes=True).then_inc(iota_ready, 1)
            pool.memset(ident[:], 0.0).then_inc(pool_seq, 1)
            pool.wait_ge(pool_seq, 1)
            pool.affine_select(out=ident[:], in_=ident[:], compare_op=ALU.not_equal, fill=1.0, base=0,
                               pattern=[[-1, P]], channel_multiplier=1).then_inc(consts_ready, 1)
            pool.memset(minus_half[:], -0.5).then_inc(consts_ready, 1)
            pool.memset(ones_f[:], 1.0).then_inc(consts_ready, 1)
            pool.memset(xt_hi[:, :, N:NP].bitcast(F32), 0.0).then_inc(consts_ready, 1)
            pool.memset(xt_lo[:, :, N:NP].bitcast(F32), 0.0).then_inc(consts_ready, 1)
            pool.memset(rwt[:], 0.0).then_inc(consts_ready, 1)
            pool.memset(e_neg_t[:, N:NP], 0.0).then_inc(consts_ready, 1)
            pool.memset(s_bc[:, N:NP], 0.0).then_inc(consts_ready, 1)
            pool.wait_ge(consts_ready, CONSTS)
            pool.wait_ge(ve_ready, 1)
            pool.tensor_tensor(rstd[:], var_eps[:], minus_half[:], ALU.pow).then_inc(rstd_ready, 1)
            for k in range(DK):
                pool.wait_ge(wg_hi_ready, k + 1)
                pool.tensor_tensor(wg_lo[:, k, :], wg_raw[:, k, :], wg_hi[:, k, :].bitcast(F32),
                                   ALU.subtract).then_inc(wg_ready, 1)

            def weight_lo(*pieces):
                for m in pieces:
                    pool.wait_ge(w_hi_ready, m + 1)
                    pool.tensor_tensor(w_lo[0][:, m, :], w_raw[0][:, m, :], w_hi[0][:, m, :].bitcast(F32),
                                       ALU.subtract).then_inc(w_ready, 1)

            for b in range(NB):
                pool.wait_ge(hg_hi_ready, b + 1)
                pool.tensor_tensor(hg_lo[:, b, :], h[:, b % 2, :], hg_hi[:, b, :].bitcast(F32),
                                   ALU.subtract).then_inc(hg_lo_ready, 1)
                if b >= 1:
                    weight_lo(2 * b - 2, 2 * b - 1)
            pool.wait_ge(rt_hi_ready, 1)
            pool.tensor_tensor(rwt_lo[:], rwt[:], rwt_hi[:].bitcast(F32), ALU.subtract).then_inc(rt_ready, 1)
            for gr in (1, 2):
                for jb in range(NB):
                    pool.wait_ge(up_ready, NB * gr + jb + 1)
                    if gr == 2:
                        pool.wait_ge(up_added, jb + 1)
                    pool.tensor_tensor(count[:, jb, 1, :], count[:, jb, 1, :], packed[:, jb, :],
                                       ALU.add).then_inc(up_added, 1)
                    if gr == 2 and jb == 0:
                        continue
                    if gr == 2:
                        pool.wait_ge(dn_added, jb + 1)
                    pool.wait_ge(dn_ready, NB * gr + jb + 1)
                    pool.tensor_tensor(count[:, jb, 0, :], count[:, jb, 0, :], count_dn[:, jb, :],
                                       ALU.add).then_inc(dn_added, 1)
            for b in range(NB):
                pool.wait_ge(ve_ready, 2 + b)
                pool.tensor_tensor(rstd[:, b:b + 1], var_eps[:, b:b + 1], minus_half[:, b:b + 1],
                                   ALU.pow).then_inc(rstd_ready, 1)
                if b < NB - 1:
                    pool.wait_ge(rstd_ready, 2 + b)
                    pool.tensor_tensor(shift[:, b:b + 1], neg_mean[:, b:b + 1], rstd[:, b:b + 1],
                                       ALU.mult).then_inc(shift_ready, 1)

        @block.scalar
        def _(act):
            def normalize(b):
                act.activation(xn[:, b, :], acc[:, b, :], ACT.Identity, bias=shift[:, b:b + 1],
                               scale=rstd[:, b:b + 1]).then_inc(xn_ready, 1)

            def transposed_hi(*blocks):
                for i in blocks:
                    b = i % NB
                    act.wait_ge(tp_done, i + 1)
                    act.activation(xt_hi[:, :, b * TB:(b + 1) * TB],
                                   r_ps[:, TP_BANK[i], 0:DK * TB].rearrange("p (k n) -> p k n", k=DK),
                                   ACT.Copy).then_inc(xt_hi_ready, 1)

            def far(*steps):
                for i in steps:
                    if i >= OH_STEPS:
                        act.wait_ge(oh_used, i - (OH_STEPS - 1))
                    for r in range(ACT_ROWS[i]):
                        n = sum(ACT_ROWS[:i]) + r
                        c = STEP - ACT_ROWS[i] + r
                        col = slice(STEP * i + c, STEP * i + c + 1)
                        if n >= 2:
                            act.wait_ge(oh_far_ready, n - 1)
                        act.activation(distance[:, n % 2, :], iota_src[:, 0:OW], ACT.Abs,
                                       bias=dst_lo_neg[:, col]).then_inc(distance_ready, 1)
                        act.wait_ge(distance_ready, n + 1)
                        act.activation(oh_dst[:, i % OH_STEPS * STEP + c, :], distance[:, n % 2, :], ACT.Relu,
                                       bias=dst_val[:, col], scale=dst_val_neg[:, col]).then_inc(oh_far_ready, 1)

            def take_counts(gr, jb):
                if jb < NB - 1:
                    act.wait_ge(cnt_done, (NB - 1) * gr + jb + 1)
                else:
                    act.wait_ge(oh_used, sum(GROUPS[:gr + 1]))
                if jb == 0 and gr == 1:
                    act.wait_ge(up_ready, NB)
                    act.wait_ge(dn_ready, NB)
                if jb == 0 and gr == 2:
                    act.wait_ge(up_added, NB)
                act.activation(packed[:, jb, :], y_ps[0:TB, jb, 0:OW], ACT.Copy).then_inc(packed_ready, 1)

            def attention_hi(jb):
                act.wait_ge(attn_ready, jb + 1)
                act.activation(attn_hi[:, jb, :], ex_lin[:, jb, :], ACT.Copy).then_inc(attn_hi_ready, 1)

            def weight_hi(*pieces):
                for m in pieces:
                    act.activation(w_hi[0][:, m, :], w_raw[0][:, m, :], ACT.Copy).then_inc(w_hi_ready, 1)

            def h_hi_part(b):
                act.wait_ge(hg_ready, b + 1)
                act.activation(hg_hi[:, b, :], h[:, b % 2, :], ACT.Copy).then_inc(hg_hi_ready, 1)

            def exponentials(jb):
                act.activation(ex_lin[:, jb, :], s_bc[:], ACT.Exp, bias=s_src_b[:, jb:jb + 1]).then_inc(ex_ready, 1)
                if jb >= 2:
                    act.wait_ge(ex_max, jb - 1)
                act.activation(ex_sl[:, jb % 2, :], s_bc[:], ACT.Exp, bias=s_src_s[:, jb:jb + 1],
                               scale=SLOPE).then_inc(ex_ready, 1)

            act.wait_ge(iota_ready, 1)
            act.wait_ge(keys_ready, 1)
            far(0, 1, 2, 3, 4, 5, 6)
            act.wait_ge(wg_in, 16)
            for k in range(DK):
                act.activation(wg_hi[:, k, :], wg_raw[:, k, :], ACT.Copy).then_inc(wg_hi_ready, 1)
            act.wait_ge(shift_ready, 1)
            for b in range(NB):
                normalize(b)
            transposed_hi(0, 1, 2)
            for jb in range(NB):
                take_counts(0, jb)
            transposed_hi(3, 4)
            far(9, 10)
            act.wait_ge(w_in[0], 32)
            for b in range(NB):
                h_hi_part(b)
                if b >= 1:
                    weight_hi(2 * b - 2, 2 * b - 1)
                if b < NB - 1:
                    far(11 + b)
            act.wait_ge(ffn_vec_in, 48)
            act.activation(rwt_hi[:], rwt[:], ACT.Copy).then_inc(rt_hi_ready, 1)
            act.wait_ge(sbc_done, 1)
            act.wait_ge(consts_ready, CONSTS)
            act.activation(s_bc[:, 0:4 * TB], r_ps[0:TB, 1, 0:4 * TB], ACT.Copy).then_inc(sbc_copied, 1)
            act.activation(s_bc[:, 4 * TB:N], r_ps[0:TB, 2, 0:TB], ACT.Copy).then_inc(sbc_copied, 1)
            far(15)
            for jb in range(NB):
                take_counts(1, jb)
            far(16)
            act.wait_ge(sbc_copied, 2)
            act.wait_ge(scores_ready, 1)
            exponentials(0)
            far(17)
            exponentials(1)
            far(18)
            for jb in range(2, NB):
                exponentials(jb)
            for jb in range(NB - 1):
                take_counts(2, jb)
            attention_hi(0)
            take_counts(2, NB - 1)
            for jb in range(1, NB):
                attention_hi(jb)
            for b in range(NB - 1):
                act.wait_ge(shift_ready, 2 + b)
                normalize(b)
                if 1 <= b <= 2:
                    transposed_hi(NB + b - 1)
                if b == 2:
                    transposed_hi(NB + 2)
            transposed_hi(NB + 3, NB + 4)
            act.wait_ge(rb_ready, 1)
            for hf, (n0, nw) in enumerate(HALVES):
                act.wait_ge(router_done, hf + 1)
                w = min(nw, N - n0)
                act.activation(e_neg_t[:, n0:n0 + w], y_ps[0:7, hf, 0:w], ACT.Exp, bias=rb_neg[:],
                               scale=-1.0).then_inc(e_neg_ready, 1)

            def expert(e, last):
                act.wait_ge(b1_ready, e + 1)
                for c in range(CH):
                    for t in range(TC):
                        j = TC * c + t
                        for hf, (n0, nw) in enumerate(HALVES):
                            u = 2 * j + hf
                            act.wait_ge(h_done, e * UNITS + u + 1)
                            if j >= 2:
                                act.wait_ge(h_ready, e * UNITS + u - 3)
                            act.activation(g[:, j % 2, n0:n0 + nw], r_ps[:, u % 3, 0:nw], ACT.Gelu,
                                           bias=b1_now[:, j:j + 1]).then_inc(gelu_done, 1)
                        if last and c == CH - 1:
                            continue
                        for m in (2 * t, 2 * t + 1):
                            s = (c + 1) % 2
                            if m == 0:
                                act.wait_ge(w_in[s], e * (32 * CH // 2) + 32 * ((c + 1) // 2 + 1))
                            if c == CH - 1 and m == PIECES - 1:
                                act.wait_ge(gelu_done, e * UNITS + UNITS)
                            act.activation(w_hi[s][:, m, :], w_raw[s][:, m, :], ACT.Copy).then_inc(w_hi_ready, 1)
                if not last:
                    act.activation(b1_now[:], b1_sb[:, bass.ds(e * HT + HT, HT)], ACT.Copy).then_inc(b1_ready, 1)

            act.activation(b1_now[:], b1_sb[:, 0:HT], ACT.Copy).then_inc(b1_ready, 1)
            with act.Fori(0, E - 1) as e:
                expert(e, False)
            expert(E - 1, True)

        @block.vector
        def _(dve):
            seq = [0]

            def landed():
                seq[0] += 1
                return seq[0]

            def layernorm_stats(b):
                dve.bn_stats(stats[:, b, :], acc[:, b, :]).then_inc(dve_seq, 1)
                dve.wait_ge(dve_seq, landed())
                dve.bn_aggr(moments[:, b, :], stats[:, b, :]).then_inc(dve_seq, 1)
                dve.wait_ge(dve_seq, landed())

            def transposed_lo(i):
                b = i % NB
                dve.wait_ge(xt_hi_ready, i + 1)
                dve.tensor_tensor(xt_lo[:, :, b * TB:(b + 1) * TB],
                                  r_ps[:, TP_BANK[i], 0:DK * TB].rearrange("p (k n) -> p k n", k=DK),
                                  xt_hi[:, :, b * TB:(b + 1) * TB].bitcast(F32), ALU.subtract).then_inc(xt_ready, 1)

            def one_hot_step(i):
                if i >= OH_STEPS:
                    dve.wait_ge(oh_used, i - (OH_STEPS - 1))
                for c in range(STEP):
                    s = i % OH_STEPS * STEP + c
                    col = slice(i * STEP + c, i * STEP + c + 1)
                    one_hot = dve.tensor_scalar(oh_src[:, s, :], iota_src[:], edge_f[:, 0, col], None, ALU.is_equal)
                    if c >= STEP - ACT_ROWS[i]:
                        one_hot.then_inc(oh_ready, 1)
                        continue
                    dve.tensor_scalar(oh_dst[:, s, :], iota_src[:, 0:OW], dst_lo[:, col], dst_val[:, col],
                                      ALU.is_equal, ALU.mult).then_inc(oh_ready, 1)

            def lower_count(gr, jb):
                dve.wait_ge(packed_ready, NB * gr + jb + 1)
                low = count[:, jb, 0, :] if gr == 0 else count_dn[:, jb, :]
                dve.tensor_scalar(low, packed[:, jb, :], int(FIELD) - 1, None, ALU.bitwise_and).then_inc(dn_ready, 1)

            def upper_count(gr, jb):
                up = count[:, jb, 1, :] if gr == 0 else packed[:, jb, :]
                dve.wait_ge(dn_ready, NB * gr + jb + 1)
                dve.tensor_scalar(up, packed[:, jb, :], FIELD_BITS, None, ALU.logical_shift_right).then_inc(up_ready, 1)

            def unpack(gr):
                for jb in range(NB):
                    lower_count(gr, jb)
                for jb in range(NB):
                    upper_count(gr, jb)

            def scores(b):
                dve.wait_ge(hg_done, b + 1)
                if b >= 2:
                    dve.wait_ge(hg_lo_ready, b - 1)
                dve.tensor_tensor(h[:, b % 2, :], r_ps[0:TB, (b + 2) % 3, :], bw_bc, ALU.add).then_inc(hg_ready, 1)
                dve.wait_ge(hg_ready, b + 1)
                for s, half in ((s_dst, 0), (s_src, 1)):
                    dve.tensor_tensor_reduce(out=scratch, in0=h[:, b % 2, :], in1=a_bc[:, half, :], scale=1.0,
                                             scalar=0.0, op0=ALU.mult, op1=ALU.add,
                                             accum_out=s[:, b:b + 1]).then_inc(dve_seq, 1)
                    dve.wait_ge(dve_seq, landed())

            def exp_max(jb):
                dve.wait_ge(ex_ready, 2 * jb + 2)
                dve.tensor_tensor(ex_lin[:, jb, :], ex_lin[:, jb, :], ex_sl[:, jb % 2, :], ALU.max).then_inc(ex_max, 1)

            dve.wait_ge(edges_in, 32)
            dve.tensor_copy(edge_f[:], edge_i[:]).then_inc(dve_seq, 1)
            dve.wait_ge(dve_seq, landed())
            dve.tensor_scalar(upper[:], edge_f[:, 1, :], float(LO_N), None, ALU.is_ge).then_inc(dve_seq, 1)
            dve.wait_ge(dve_seq, landed())
            dve.scalar_tensor_tensor(dst_lo[:], upper[:], -float(LO_N), edge_f[:, 1, :], ALU.mult,
                                     ALU.add).then_inc(dve_seq, 1)
            landed()
            dve.tensor_scalar(dst_val[:], upper[:], FIELD - 1.0, 1.0, ALU.mult, ALU.add).then_inc(dve_seq, 1)
            landed()
            dve.wait_ge(dve_seq, seq[0])
            dve.tensor_scalar(dst_lo_neg[:], dst_lo[:], -1.0, None, ALU.mult)
            dve.tensor_scalar(dst_val_neg[:], dst_val[:], -1.0, None, ALU.mult).then_inc(keys_ready, 1)
            dve.wait_ge(iota_ready, 1)
            one_hot_step(0)
            for b in range(NB):
                if b < 4:
                    one_hot_step(1 + b)
                if b == 0:
                    dve.wait_ge(x_in, 16)
                dve.bn_stats(stats[:, b, :], acc[:, b, :]).then_inc(dve_seq, 1)
                landed()
            dve.wait_ge(dve_seq, seq[0])
            for b in range(NB):
                dve.bn_aggr(moments[:, b, :], stats[:, b, :]).then_inc(dve_seq, 1)
                landed()
            dve.wait_ge(dve_seq, seq[0])
            dve.tensor_scalar(var_eps[:], moments[:, :, 1], EPS, None, ALU.add).then_inc(ve_ready, 1)
            one_hot_step(5)
            dve.wait_ge(rstd_ready, 1)
            dve.scalar_tensor_tensor(shift[:], moments[:, :, 0], -1.0, rstd[:], ALU.mult, ALU.mult).then_inc(shift_ready, 1)
            one_hot_step(6)
            one_hot_step(7)
            one_hot_step(8)
            for b in range(3):
                transposed_lo(b)
            unpack(0)
            transposed_lo(3)
            transposed_lo(4)
            dve.wait_ge(vec_in, 64)
            one_hot_step(9)
            for b in range(NB):
                scores(b)
                if b < NB - 1:
                    one_hot_step(10 + b)
            for b in range(NB):
                dve.tensor_scalar(diag[:, b, :], ident[0:TB, 0:TB], s_dst[:, b:b + 1], None,
                                  ALU.mult).then_inc(diag_ready, 1)
            dve.tensor_scalar(s_src_b[:], s_src[:], ba_bc[:, 0:1], None, ALU.add).then_inc(dve_seq, 1)
            dve.wait_ge(dve_seq, landed())
            dve.tensor_scalar(s_src_s[:], s_src_b[:], SLOPE, None, ALU.mult).then_inc(scores_ready, 1)
            one_hot_step(14)
            one_hot_step(15)
            unpack(1)
            one_hot_step(16)
            one_hot_step(17)
            exp_max(0)
            one_hot_step(18)
            exp_max(1)
            one_hot_step(19)
            exp_max(2)
            exp_max(3)
            def weights(jb):
                dve.wait_ge(up_added, NB + jb + 1)
                if jb == 0:
                    dve.wait_ge(first_dn_added, 1)
                else:
                    dve.wait_ge(dn_added, NB + jb)
                w = ex_lin[:, jb, :].rearrange("p (f n) -> p f n", f=2)
                dve.scalar_tensor_tensor(w, w, FLT_MAX, count[:, jb, :, 0:LO_N], ALU.min, ALU.mult).then_inc(attn_ready, 1)

            def weights_lo(jb):
                dve.wait_ge(attn_hi_ready, jb + 1)
                dve.tensor_tensor(attn_lo[:, jb, :], ex_lin[:, jb, :], attn_hi[:, jb, :].bitcast(F32),
                                  ALU.subtract).then_inc(attn_lo_ready, 1)

            dve.wait_ge(dn_added, NB)
            lower_count(2, 0)
            upper_count(2, 0)
            dve.tensor_tensor(count[:, 0, 0, :], count[:, 0, 0, :], count_dn[:, 0, :],
                              ALU.add).then_inc(first_dn_added, 1)
            exp_max(4)
            for jb in range(NB):
                if jb + 1 < NB:
                    lower_count(2, jb + 1)
                if jb == 1:
                    dve.wait_ge(oh_used, sum(GROUPS))
                if jb >= 1:
                    weights_lo(jb - 1)
                if jb + 1 < NB:
                    upper_count(2, jb + 1)
                weights(jb)
            weights_lo(NB - 1)
            dve.wait_ge(ffn_vec_in, 48)
            dve.tensor_scalar(rb_neg[:], rb_col[:], -1.0, None, ALU.mult).then_inc(rb_ready, 1)
            def second_layernorm(b):
                dve.wait_ge(agg_done, b + 1)
                dve.scalar_tensor_tensor(acc[:, b, :], y_ps[0:TB, b, :], rden[:, b:b + 1], acc[:, b, :],
                                         ALU.mult, ALU.add).then_inc(y_added, 1)
                dve.wait_ge(y_added, b + 1)
                layernorm_stats(b)
                if b < NB - 1:
                    dve.tensor_scalar(neg_mean[:, b:b + 1], moments[:, b, 0:1], -1.0, None, ALU.mult)
                dve.tensor_scalar(var_eps[:, b:b + 1], moments[:, b, 1:2], EPS, None, ALU.add).then_inc(ve_ready, 1)

            def denominators(first, last):
                blocks = slice(first, last)
                dve.wait_ge(den_read, last)
                dve.scalar_tensor_tensor(den_safe[:, blocks], den[:, blocks], 0.0, den[:, blocks],
                                         ALU.is_equal, ALU.add).then_inc(dve_seq, 1)
                dve.wait_ge(dve_seq, landed())
                dve.reciprocal(rden[:, blocks], den_safe[:, blocks]).then_inc(dve_seq, 1)
                dve.wait_ge(dve_seq, landed())

            for b in range(3):
                dve.wait_ge(den_done, b + 1)
                dve.tensor_copy(den[:, b:b + 1], r_ps[0:TB, b, 0:1]).then_inc(den_read, 1)
            denominators(0, 3)
            for b in range(3):
                second_layernorm(b)
            dve.wait_ge(den_done, NB)
            for ib in (3, 4):
                dve.tensor_copy(den[:, ib:ib + 1], r_ps[0:TB, 0, 2 * ib:2 * ib + 1]).then_inc(den_read, 1)
            denominators(3, NB)
            second_layernorm(3)
            for b in range(3):
                transposed_lo(NB + b)
            second_layernorm(4)
            transposed_lo(NB + 3)
            dve.wait_ge(rstd_ready, 1 + NB)
            dve.tensor_scalar(xn[:, NB - 1, :], acc[:, NB - 1, :], moments[:, NB - 1, 0:1], rstd[:, NB - 1:NB],
                              ALU.subtract, ALU.mult).then_inc(xn_ready, 1)
            transposed_lo(NB + 4)

            def leaf_probabilities():
                dve.wait_ge(tree_done, 1)
                dve.tensor_scalar(one_plus[:], y_ps[0:TB, 2, 0:8 * NB].rearrange("p (b n) -> p b n", b=NB)[:, :, 0:7], 1.0,
                                  None, ALU.add).then_inc(tree_read, 1)
                dve.wait_ge(tree_read, 1)
                dve.reciprocal(prob[:, :, :, 1], one_plus[:]).then_inc(dve_seq, 1)
                dve.wait_ge(dve_seq, landed())
                dve.tensor_scalar(prob[:, :, :, 0], prob[:, :, :, 1], -1.0, 1.0, ALU.mult, ALU.add).then_inc(dve_seq, 1)
                dve.wait_ge(dve_seq, landed())
                for m in range(4):
                    dve.tensor_tensor(pair[:, :, m], prob[:, :, 0, m // 2], prob[:, :, 1 + m // 2, m % 2],
                                      ALU.mult).then_inc(dve_seq, 1)
                    landed()
                dve.wait_ge(dve_seq, seq[0])
                for n in range(E):
                    dve.tensor_tensor(leaf[:, :, n], pair[:, :, n // 2], prob[:, :, 3 + n // 2, n % 2],
                                      ALU.mult).then_inc(dve_seq, 1)
                    landed()
                dve.wait_ge(dve_seq, seq[0])

            def expert(e, first, last):
                for c in range(CH):
                    for t in range(TC):
                        j = TC * c + t
                        for hf, (n0, nw) in enumerate(HALVES):
                            u = 2 * j + hf
                            cols = slice(n0, n0 + nw)
                            dve.wait_ge(gelu_done, e * UNITS + u + 1)
                            if hf == 0 and j >= 2:
                                dve.wait_ge(l2_done, e * (HT - 1) + j - 1)
                            dve.tensor_copy(h_hi[:, j % 2, cols], g[:, j % 2, cols]).then_inc(h_hi_ready, 1)
                            dve.wait_ge(h_hi_ready, e * UNITS + u + 1)
                            dve.tensor_tensor(h_lo[:, j % 2, cols], g[:, j % 2, cols],
                                              h_hi[:, j % 2, cols].bitcast(F32), ALU.subtract).then_inc(h_ready, 1)
                        if first and j == 0:
                            leaf_probabilities()
                        if 2 <= j < 2 + NB:
                            b = j - 2
                            if b == 0:
                                dve.wait_ge(b2_in, 16)
                                dve.wait_ge(y_added, e * NB + NB)
                            dve.scalar_tensor_tensor(acc[:, b, :], b2_bc[:, bass.ds(e, 1), :].rearrange("p e d -> p (e d)"),
                                                     leaf[:, b, bass.ds(e, 1)], acc[:, b, :],
                                                     ALU.mult, ALU.add).then_inc(b2_added, 1)
                        if last and c == CH - 1:
                            continue
                        for m in (2 * t, 2 * t + 1):
                            s = (c + 1) % 2
                            dve.wait_ge(w_hi_ready, e * (CH * PIECES) + PIECES * (c + 1) + m + 1)
                            dve.tensor_tensor(w_lo[s][:, m, :], w_raw[s][:, m, :], w_hi[s][:, m, :].bitcast(F32),
                                              ALU.subtract).then_inc(w_ready, 1)
                dve.wait_ge(b2_added, e * NB + NB)
                for b in range(NB):
                    dve.wait_ge(y_done, e * NB + b + 1)
                    dve.scalar_tensor_tensor(acc[:, b, :], y_ps[0:TB, b, :], leaf[:, b, bass.ds(e, 1)], acc[:, b, :],
                                             ALU.mult, ALU.add).then_inc(y_added, 1)

            expert(0, True, False)
            with dve.Fori(1, E - 1) as e:
                expert(e, False, False)
            expert(E - 1, False, True)

        @block.tensor
        def _(pe):
            def product(out_ap, lhs, rhs, start, stop):
                pe.matmul(out_ap, lhs[0], rhs[0], start=start, stop=False)
                pe.matmul(out_ap, lhs[0], rhs[1], start=False, stop=False)
                return pe.matmul(out_ap, lhs[1], rhs[0], start=False, stop=stop)

            def transpose_block(i):
                b = i % NB
                pe.wait_ge(xn_ready, i + 1)
                for k in range(DK):
                    m = pe.transpose(r_ps[:, TP_BANK[i], k * TB:(k + 1) * TB], xn[:, b, k * P:(k + 1) * P],
                                     ident[0:TB, 0:TB])
                m.then_inc(tp_done, 1)

            def count_chunk(i, c, jb, start=False, stop=False):
                s = i % OH_STEPS * STEP + c
                return pe.matmul(y_ps[0:TB, jb, 0:OW], oh_src[:, s, jb * TB:(jb + 1) * TB], oh_dst[:, s, :],
                                 start=start, stop=stop)

            def count_first_step():
                for c in range(STEP):
                    pe.wait_ge(oh_ready, c + 1)
                    if c == STEP - ACT_ROWS[0]:
                        pe.wait_ge(oh_far_ready, ACT_ROWS[0])
                    for jb in range(NB):
                        m = count_chunk(0, c, jb, start=c == 0)
                m.then_inc(oh_used, 1)

            def count_steps(*steps, gr, first=False, last=False):
                i = steps[-1]
                pe.wait_ge(oh_ready, (i + 1) * STEP)
                pe.wait_ge(oh_far_ready, sum(ACT_ROWS[:i + 1]))
                for jb in range(NB):
                    if gr >= 1 and first:
                        pe.wait_ge(packed_ready, NB * (gr - 1) + jb + 1)
                    for i in steps:
                        for c in range(STEP):
                            m = count_chunk(i, c, jb, start=first and c == 0, stop=last and i == steps[-1] and c == STEP - 1)
                    if last and jb < NB - 1:
                        m.then_inc(cnt_done, 1)
                m.then_inc(oh_used, len(steps))

            def hidden_graph(b):
                if b == 0:
                    pe.wait_ge(wg_ready, DK)
                if b < 3:
                    pe.wait_ge(xt_ready, b + 3)
                else:
                    pe.wait_ge(hg_ready, b - 2)
                for k in range(DK):
                    cols = slice(b * TB, (b + 1) * TB)
                    m = product(r_ps[0:TB, (b + 2) % 3, :], (xt_hi[:, k, cols], xt_lo[:, k, cols]),
                                (wg_hi[:, k, :], wg_lo[:, k, :]), k == 0, k == DK - 1)
                m.then_inc(hg_done, 1)

            pe.wait_ge(iota_ready, 1)
            for _ in range(WARM_UP):
                pe.matmul(r_ps[0:TB, 1, :], iota_src[:, 0:TB], iota_src[:, 0:512], start=True, stop=True)
            pe.wait_ge(consts_ready, CONSTS)
            count_first_step()
            for i in range(1, 6):
                count_steps(i, gr=0)
            for b in range(3):
                transpose_block(b)
            count_steps(6, gr=0, last=True)
            for b in (3, 4):
                pe.wait_ge(xt_ready, b - 2)
                transpose_block(b)
            for b in range(NB):
                hidden_graph(b)
                count_steps(7 + b, gr=1, first=b == 0)
            count_steps(12, gr=1)
            pe.wait_ge(hg_ready, NB - 1)
            for b in range(NB):
                pe.wait_ge(diag_ready, b + 1)
                m = pe.matmul(r_ps[0:TB, 1 + b // 4, (b % 4) * TB:(b % 4 + 1) * TB], ones_f[:], diag[:, b, :],
                              start=True, stop=True)
            m.then_inc(sbc_done, 1)
            count_steps(13, gr=1, last=True)
            count_steps(14, gr=2, first=True)
            for i in range(15, 18):
                count_steps(i, gr=2)
            count_steps(18, 19, gr=2, last=True)

            def attend(ib, jb, parts):
                cols = slice(ib * TB, (ib + 1) * TB)
                if 0 in parts:
                    pe.matmul(y_ps[0:TB, ib, :], attn_hi[:, jb, cols], hg_hi[:, jb, :], start=jb == 0, stop=False)
                    m = pe.matmul(y_ps[0:TB, ib, :], attn_hi[:, jb, cols], hg_lo[:, jb, :], start=False, stop=False)
                if 1 in parts:
                    m = pe.matmul(y_ps[0:TB, ib, :], attn_lo[:, jb, cols], hg_hi[:, jb, :], start=False,
                                  stop=jb == NB - 1)
                return m

            def denominator(ib, jb, out_ap):
                return pe.matmul(out_ap, ex_lin[:, jb, ib * TB:(ib + 1) * TB], ones_f[:, 0:2],
                                 start=jb == 0, stop=jb == NB - 1)

            pe.wait_ge(hg_lo_ready, NB)
            pe.wait_ge(sbc_copied, 2)
            for jb in range(NB):
                pe.wait_ge(attn_ready, jb + 1)
                for ib in range(3):
                    m = denominator(ib, jb, r_ps[0:TB, ib, 0:2])
                    if jb == NB - 1:
                        m.then_inc(den_done, 1)
                pe.wait_ge(attn_hi_ready, jb + 1)
                for ib in range(3):
                    pe.wait_ge(packed_ready, 2 * NB + ib + 1)
                    attend(ib, jb, (0,))
                pe.wait_ge(attn_lo_ready, jb + 1)
                for ib in range(3):
                    m = attend(ib, jb, (1,))
                    if jb == NB - 1:
                        m.then_inc(agg_done, 1)
            pe.wait_ge(den_read, 3)
            for ib in (3, 4):
                for jb in range(NB):
                    m = denominator(ib, jb, r_ps[0:TB, 0, 2 * ib:2 * ib + 2])
                m.then_inc(den_done, 1)
            pe.wait_ge(packed_ready, 3 * NB)
            for jb in range(NB):
                m = attend(3, jb, (0, 1))
            m.then_inc(agg_done, 1)
            transpose_block(NB)
            transpose_block(NB + 1)
            for jb in range(NB):
                if jb == 3:
                    pe.wait_ge(den_read, NB)
                    transpose_block(NB + 2)
                m = attend(4, jb, (0, 1))
            m.then_inc(agg_done, 1)

            def router(hf):
                n0, nw = HALVES[hf]
                pe.wait_ge(y_added, hf + 1)
                for k in range(DK):
                    cols = slice(n0, n0 + nw)
                    m = product(y_ps[:, hf, 0:nw], (rwt_hi[:, k, :], rwt_lo[:, k, :]),
                                (xt_hi[:, k, cols], xt_lo[:, k, cols]), k == 0, k == DK - 1)
                m.then_inc(router_done, 1)

            pe.wait_ge(xt_ready, NB + 1)
            transpose_block(NB + 3)

            def tree():
                pe.wait_ge(y_added, 3)
                pe.wait_ge(e_neg_ready, 2)
                for b in range(NB):
                    m = pe.transpose(y_ps[0:TB, 2, 8 * b:8 * b + 7], e_neg_t[:, b * TB:(b + 1) * TB], ident[0:7, 0:7])
                m.then_inc(tree_done, 1)

            def hidden(e, j, halves=(0, 1)):
                s, t = (j // TC) % 2, j % TC
                if t == 0:
                    pe.wait_ge(w_ready, e * (CH * PIECES) + PIECES * (j // TC) + DK)
                for hf in halves:
                    n0, nw = HALVES[hf]
                    u = 2 * j + hf
                    if u >= 3:
                        pe.wait_ge(gelu_done, e * UNITS + u - 2)
                    for k in range(DK):
                        cols = slice(n0, n0 + nw)
                        wc = slice(t * P, (t + 1) * P)
                        m = product(r_ps[:, u % 3, 0:nw], (w_hi[s][:, k, wc], w_lo[s][:, k, wc]),
                                    (xt_hi[:, k, cols], xt_lo[:, k, cols]), k == 0, k == DK - 1)
                    m.then_inc(h_done, 1)

            def output(e, j):
                s, t = (j // TC) % 2, j % TC
                pe.wait_ge(w_ready, e * (CH * PIECES) + PIECES * (j // TC) + DK + t + 1)
                pe.wait_ge(h_ready, e * UNITS + 2 * j + 2)
                if j == 0:
                    pe.wait_ge(y_added, e * NB + NB)
                    pe.wait_ge(tree_read, 1)
                for b in range(NB):
                    cols = slice(b * TB, (b + 1) * TB)
                    m = product(y_ps[0:TB, b, :], (h_hi[:, j % 2, cols], h_lo[:, j % 2, cols]),
                                (w_hi[s][:, DK + t, :], w_lo[s][:, DK + t, :]), j == 0, j == HT - 1)
                    if j == HT - 1:
                        m.then_inc(y_done, 1)
                if j < HT - 1:
                    m.then_inc(l2_done, 1)

            def expert_rest(e):
                for j in range(1, HT):
                    if j >= 2:
                        hidden(e, j)
                    output(e, j - 1)
                output(e, HT - 1)

            pe.wait_ge(xt_ready, NB + 3)
            hidden(0, 0, (0,))
            transpose_block(NB + 4)
            pe.wait_ge(rt_ready, 1)
            router(0)
            pe.wait_ge(xt_ready, NB + 5)
            router(1)
            hidden(0, 0, (1,))
            tree()
            hidden(0, 1)
            expert_rest(0)
            with pe.Fori(1, E) as e:
                hidden(e, 0)
                hidden(e, 1)
                expert_rest(e)


TP_BANK = (0, 1, 2, 0, 1, 1, 2, 0, 1, 2)


def kernel(x, src, dst, L0_gnn_W, L0_gnn_b_w, L0_gnn_a, L0_gnn_b_a, L0_ffn_rw, L0_ffn_rb, L0_ffn_w1, L0_ffn_b1,
           L0_ffn_w2, L0_ffn_b2):
    import numpy as np
    import concourse.bacc as bacc
    from concourse.bass_utils import run_bass_kernel_spmd

    rw = np.asarray(L0_ffn_rw)
    rw_t = rw.reshape(rw.shape[0], DK, P).transpose(2, 1, 0).reshape(P, -1)
    b1_t = np.asarray(L0_ffn_b1).reshape(E * HT, P).T
    ins = {
        "x": x, "src": src, "dst": dst, "w_gnn": L0_gnn_W, "b_w": L0_gnn_b_w, "a_vec": L0_gnn_a,
        "b_a": np.asarray(L0_gnn_b_a).reshape(1), "rw_t": rw_t, "rb": L0_ffn_rb, "w1": L0_ffn_w1, "b1_t": b1_t,
        "w2": L0_ffn_w2, "b2": L0_ffn_b2,
    }
    nc = bacc.Bacc("TRN2", target_bir_lowering=False, num_devices=1)
    arrays, args = {}, {}
    for name, value in ins.items():
        value = np.ascontiguousarray(value)
        arrays[f"in_{name}"] = value
        args[name] = nc.dram_tensor(f"in_{name}", value.shape, mybir.dt.from_np(value.dtype), kind="ExternalInput").ap()
    args["out"] = nc.dram_tensor("out_x", (N, D), F32, kind="ExternalOutput").ap()
    gnn_ffn_kernel(nc, **args)
    result = run_bass_kernel_spmd(nc, [arrays], core_ids=[0])
    return result.results[0]["out_x"]
```
